# Optimizing a Trainium2 kernel written in Bass

```python
import numpy as np
import jax
import jax.numpy as jnp

def _softmax(x, axis=-1):
    return jax.nn.softmax(x, axis=axis)

def _gelu(x):
    return jax.nn.gelu(x, approximate=True)

def _silu(x):
    return jax.nn.silu(x)

def _sigmoid(x):
    return jax.nn.sigmoid(x)

def _layernorm(x, axis=-1, eps=1e-05):
    m = jnp.mean(x, axis=axis, keepdims=True)
    v = jnp.var(x, axis=axis, keepdims=True)
    return (x - m) / jnp.sqrt(v + eps)

def _scatter_add(tgt, idx, src, axis=0):
    return tgt.at[idx].add(src)

def _segment_sum(src, seg, n):
    return jax.ops.segment_sum(src, seg, n)
kernel_name = 'mk_gnn_resnorm_d4_gnn_r8_dbb86a'

def setup_inputs(seed: int=0):
    np.random.seed(seed)
    _w = jnp.asarray

    def _rec_inputs():
        import jax
        import jax.numpy as jnp
        _gk = jax.random.key(seed)
        x = -0.0003713 + 1 * jax.random.normal(jax.random.fold_in(_gk, 1), (12500, 128), jnp.float32)
        _s = jax.random.randint(jax.random.fold_in(_gk, 2), (100000,), 0, 12500, jnp.int32)
        _d = jax.random.randint(jax.random.fold_in(_gk, 3), (100000,), 0, 12500, jnp.int32)
        _loop = jnp.arange(12500, dtype=jnp.int32)
        src = jnp.concatenate([_s, _d, _loop])
        dst = jnp.concatenate([_d, _s, _loop])
        _o = jnp.argsort(dst, stable=True)
        src = src[_o]
        dst = dst[_o]
        edge_attr_128 = 5.93493e-05 + 1.00006 * jax.random.normal(jax.random.fold_in(_gk, 12), (212500, 128), jnp.float32)
        edge_attr_32 = 0.000196303 + 1.00016 * jax.random.normal(jax.random.fold_in(_gk, 13), (212500, 32), jnp.float32)
        return (x, src, dst, edge_attr_128, edge_attr_32)
    x, src, dst, edge_attr_128, edge_attr_32 = _rec_inputs()

    def _L0_gnn_setup():
        import jax, jax.numpy as jnp
        import numpy as np
        K = 3
        key = jax.random.key(seed)
        k1, k2 = jax.random.split(key)
        N, E, D = (12500, 400000, 128)
        h_local = jax.random.normal(k1, (N, D), dtype=jnp.float32)
        edge_list = jax.random.randint(k2, (2, E), 0, N, dtype=jnp.int64)
        return {'h_local': h_local, 'edge_list': edge_list, 'num_nodes': N}
    _L0_gnn_all = _L0_gnn_setup()
    _L0_gnn_in = {k: v for k, v in _L0_gnn_all.items() if k in ()}
    del _L0_gnn_all

    def _L1_gnn_setup():
        import jax, jax.numpy as jnp
        import numpy as np
        N, E, IN_DIM, H, D = (12500, 200000, 128, 4, 32)
        key = jax.random.key(seed)
        ks = jax.random.split(key, 8)
        glorot = lambda k, shape: jax.random.uniform(k, shape, jnp.float32, -1.0, 1.0) * np.sqrt(6.0 / (shape[0] + shape[1]))
        return {'x': jax.random.normal(ks[0], (N, IN_DIM), jnp.float32), 'row': jax.random.randint(ks[1], (E,), 0, N, jnp.int32), 'col': jax.random.randint(ks[2], (E,), 0, N, jnp.int32), 'W_l': glorot(ks[3], (IN_DIM, H * D)), 'W_r': glorot(ks[4], (IN_DIM, H * D)), 'a1w': glorot(ks[5], (IN_DIM, H)), 'a2w': glorot(ks[6], (IN_DIM, H)), 'bias': jnp.zeros((H * D,), jnp.float32)}
    _L1_gnn_all = _L1_gnn_setup()
    _L1_gnn_in = {k: v for k, v in _L1_gnn_all.items() if k in ('W_l', 'W_r', 'a1w', 'a2w', 'bias')}
    del _L1_gnn_all

    def _L2_gnn_setup():
        import jax, jax.numpy as jnp
        import numpy as np
        N, E = (6250, 100000)
        NODE_DIM, EDGE_DIM, HIDDEN_DIM = (128, 32, 128)
        LN_EPS = 1e-05
        key = jax.random.key(seed)
        ks = jax.random.split(key, 10)

        def lin(k, fan_in, fan_out):
            bound = 1.0 / np.sqrt(fan_in)
            kw, kb = jax.random.split(k)
            W = jax.random.uniform(kw, (fan_out, fan_in), jnp.float32, -bound, bound)
            b = jax.random.uniform(kb, (fan_out,), jnp.float32, -bound, bound)
            return (W, b)
        x = jax.random.normal(ks[0], (N, NODE_DIM), jnp.float32)
        edge_index = jax.random.randint(ks[1], (2, E), 0, N, jnp.int64)
        edge_attr = jax.random.normal(ks[2], (E, EDGE_DIM), jnp.float32)
        W1, b1 = lin(ks[3], 2 * NODE_DIM + EDGE_DIM, HIDDEN_DIM)
        W2, b2 = lin(ks[4], HIDDEN_DIM, HIDDEN_DIM)
        Wu, bu = lin(ks[5], HIDDEN_DIM, NODE_DIM)
        gamma = jnp.ones((NODE_DIM,), jnp.float32)
        beta = jnp.zeros((NODE_DIM,), jnp.float32)
        return {'x': x, 'edge_attr': edge_attr, 'W1': W1, 'b1': b1, 'W2': W2, 'b2': b2, 'Wu': Wu, 'bu': bu, 'gamma': gamma, 'beta': beta, 'edge_index': edge_index}
    _L2_gnn_all = _L2_gnn_setup()
    _L2_gnn_in = {k: v for k, v in _L2_gnn_all.items() if k in ('W1', 'b1', 'W2', 'b2', 'Wu', 'bu', 'gamma', 'beta')}
    del _L2_gnn_all

    def _L3_gnn_setup():
        import jax, jax.numpy as jnp
        import numpy as np
        N_NODES = 12500
        N_EDGES = 75000
        D = 128
        H = 256
        LN_EPS = 1e-05
        key = jax.random.key(seed)
        ks = jax.random.split(key, 8)
        x = jax.random.normal(ks[0], (N_NODES, D), dtype=jnp.float32)
        edge_index = jax.random.randint(ks[1], (2, N_EDGES), 0, N_NODES, dtype=jnp.int64)
        edge_attr = jax.random.normal(ks[2], (N_EDGES, D), dtype=jnp.float32)
        s1 = 1.0 / np.sqrt(H)
        s2 = 1.0 / np.sqrt(H)
        W1 = jax.random.uniform(ks[3], (H, H), jnp.float32, -s1, s1)
        b1 = jax.random.uniform(ks[4], (H,), jnp.float32, -s1, s1)
        W2 = jax.random.uniform(ks[5], (H, D), jnp.float32, -s2, s2)
        b2 = jax.random.uniform(ks[6], (D,), jnp.float32, -s2, s2)
        ln_gamma = jnp.ones((D,), jnp.float32)
        ln_beta = jnp.zeros((D,), jnp.float32)
        return {'x': x, 'edge_index': edge_index, 'edge_attr': edge_attr, 'W1': W1, 'b1': b1, 'W2': W2, 'b2': b2, 'ln_gamma': ln_gamma, 'ln_beta': ln_beta}
    _L3_gnn_all = _L3_gnn_setup()
    _L3_gnn_in = {k: v for k, v in _L3_gnn_all.items() if k in ('W1', 'b1', 'W2', 'b2', 'ln_gamma', 'ln_beta')}
    del _L3_gnn_all
    return {'x': x, 'src': src, 'dst': dst, 'edge_attr_128': edge_attr_128, 'edge_attr_32': edge_attr_32, 'L1_gnn_W_l': _L1_gnn_in['W_l'], 'L1_gnn_W_r': _L1_gnn_in['W_r'], 'L1_gnn_a1w': _L1_gnn_in['a1w'], 'L1_gnn_a2w': _L1_gnn_in['a2w'], 'L1_gnn_bias': _L1_gnn_in['bias'], 'L2_gnn_W1': _L2_gnn_in['W1'], 'L2_gnn_b1': _L2_gnn_in['b1'], 'L2_gnn_W2': _L2_gnn_in['W2'], 'L2_gnn_b2': _L2_gnn_in['b2'], 'L2_gnn_Wu': _L2_gnn_in['Wu'], 'L2_gnn_bu': _L2_gnn_in['bu'], 'L2_gnn_gamma': _L2_gnn_in['gamma'], 'L2_gnn_beta': _L2_gnn_in['beta'], 'L3_gnn_W1': _L3_gnn_in['W1'], 'L3_gnn_b1': _L3_gnn_in['b1'], 'L3_gnn_W2': _L3_gnn_in['W2'], 'L3_gnn_b2': _L3_gnn_in['b2'], 'L3_gnn_ln_gamma': _L3_gnn_in['ln_gamma'], 'L3_gnn_ln_beta': _L3_gnn_in['ln_beta']}

def reference(x, src, dst, edge_attr_128, edge_attr_32, L1_gnn_W_l, L1_gnn_W_r, L1_gnn_a1w, L1_gnn_a2w, L1_gnn_bias, L2_gnn_W1, L2_gnn_b1, L2_gnn_W2, L2_gnn_b2, L2_gnn_Wu, L2_gnn_bu, L2_gnn_gamma, L2_gnn_beta, L3_gnn_W1, L3_gnn_b1, L3_gnn_W2, L3_gnn_b2, L3_gnn_ln_gamma, L3_gnn_ln_beta):
    import jax
    import jax.numpy as jnp

    def _L0_gnn_ref(h_local, edge_list, num_nodes):
        import jax, jax.numpy as jnp
        import numpy as np
        K = 3
        N = num_nodes
        loops = jnp.broadcast_to(jnp.arange(N, dtype=edge_list.dtype)[None, :], (2, N))
        ei = jnp.concatenate([edge_list, loops], axis=1)
        row, col = (ei[0], ei[1])
        deg = jax.ops.segment_sum(jnp.ones_like(row, dtype=h_local.dtype), row, num_segments=N)
        deg_inv_sqrt = jnp.where(deg > 0, jax.lax.rsqrt(jnp.maximum(deg, 1.0)), 0.0)
        w = deg_inv_sqrt[row] * deg_inv_sqrt[col]

        def spmm(H):
            return jax.ops.segment_sum(w[:, None] * H[col], row, num_segments=N)
        H = h_local
        for _ in range(K):
            H = spmm(H)
        return H

    def _L1_gnn_ref(x, row, col, W_l, W_r, a1w, a2w, bias):
        import jax, jax.numpy as jnp
        import numpy as np
        N, E, IN_DIM, H, D = (12500, 200000, 128, 4, 32)
        n = x.shape[0]
        x_l = (x @ W_l).reshape(n, H, D)
        x_r = x @ W_r
        attn = jax.nn.leaky_relu((x @ a1w)[row] + (x @ a2w)[col], 0.2)
        m = jax.ops.segment_max(attn, row, num_segments=n)
        e = jnp.exp(attn - m[row])
        s = jax.ops.segment_sum(e, row, num_segments=n)
        attn_d = e / s[row]
        msgs = attn_d[:, :, None] * x_l[col]
        out = jax.ops.segment_sum(msgs, row, num_segments=n).reshape(n, H * D)
        return out + x_r + bias

    def _L2_gnn_ref(x, edge_attr, W1, b1, W2, b2, Wu, bu, gamma, beta, edge_index):
        import jax, jax.numpy as jnp
        import numpy as np
        N, E = (6250, 100000)
        NODE_DIM, EDGE_DIM, HIDDEN_DIM = (128, 32, 128)
        LN_EPS = 1e-05
        src, dst = (edge_index[0], edge_index[1])
        msg_input = jnp.concatenate([x[src], x[dst], edge_attr], axis=-1)
        h = jax.nn.relu(msg_input @ W1.T + b1)
        messages = h @ W2.T + b2
        agg = jax.ops.segment_sum(messages, dst, num_segments=x.shape[0])
        upd = jax.nn.relu(agg @ Wu.T + bu)
        y = x + upd
        mean = jnp.mean(y, axis=-1, keepdims=True)
        var = jnp.mean(jnp.square(y - mean), axis=-1, keepdims=True)
        return (y - mean) * jax.lax.rsqrt(var + LN_EPS) * gamma + beta

    def _L3_gnn_ref(x, edge_index, edge_attr, W1, b1, W2, b2, ln_gamma, ln_beta):
        import jax, jax.numpy as jnp
        import numpy as np
        N_NODES = 12500
        N_EDGES = 75000
        D = 128
        H = 256
        LN_EPS = 1e-05
        i = edge_index[0]
        agg = jax.ops.segment_sum(edge_attr, i, num_segments=x.shape[0])
        h = jnp.concatenate([x, agg], axis=-1)
        h = jax.nn.silu(h @ W1 + b1)
        h = h @ W2 + b2
        mu = jnp.mean(h, axis=-1, keepdims=True)
        var = jnp.mean(jnp.square(h - mu), axis=-1, keepdims=True)
        h = (h - mu) * jax.lax.rsqrt(var + LN_EPS) * ln_gamma + ln_beta
        return h + x
    edge_index = jnp.stack([src, dst])
    x = _layernorm(x + _L0_gnn_ref(x, edge_index, 12500), axis=-1)
    x = _layernorm(x + _L1_gnn_ref(x, src, dst, L1_gnn_W_l, L1_gnn_W_r, L1_gnn_a1w, L1_gnn_a2w, L1_gnn_bias), axis=-1)
    x = _layernorm(x + _L2_gnn_ref(x, edge_attr_32, L2_gnn_W1, L2_gnn_b1, L2_gnn_W2, L2_gnn_b2, L2_gnn_Wu, L2_gnn_bu, L2_gnn_gamma, L2_gnn_beta, edge_index), axis=-1)
    x = _layernorm(x + _L3_gnn_ref(x, edge_index, edge_attr_128, L3_gnn_W1, L3_gnn_b1, L3_gnn_W2, L3_gnn_b2, L3_gnn_ln_gamma, L3_gnn_ln_beta), axis=-1)
    return x

_drawn_inputs = setup_inputs


def setup_inputs(seed=0):
    import zlib

    import numpy as np

    out = dict(_drawn_inputs(seed))
    spreads = {'L1_gnn_bias': (0.0, 0.1),
     'L2_gnn_gamma': (1.0, 0.2),
     'L2_gnn_beta': (0.0, 0.1),
     'L3_gnn_ln_gamma': (1.0, 0.2),
     'L3_gnn_ln_beta': (0.0, 0.1)}
    factors = {'L2_gnn_bu': 4.506, 'L3_gnn_b1': 5.302}
    for name, (base, spread) in spreads.items():
        noise = np.random.default_rng([zlib.crc32(name.encode()), seed]).standard_normal(out[name].shape)
        drawn = base * np.exp(spread * noise) if base else spread * noise
        out[name] = jnp.asarray(drawn.astype(out[name].dtype))
    for name, factor in factors.items():
        out[name] = (out[name] * factor).astype(out[name].dtype)
    return out
```

```python
from contextlib import ExitStack

import concourse.bass as bass
from concourse import mybir

ALU = mybir.AluOpType
ACT = mybir.ActivationFunctionType
AX = mybir.AxisListType.X
F32 = mybir.dt.float32
I32 = mybir.dt.int32
I16 = mybir.dt.int16
BF16 = mybir.dt.bfloat16
ds = bass.ds

P = 128
N, E, D, DE = 12500, 212500, 128, 32
H, HD = 4, 32
NB = -(-N // P)
NP = NB * P
LASTN = N - (NB - 1) * P
FC = E // P
REST = E - FC * P
COLS = FC + 1
ROW_BITS = 7
TP = 1760
SB = 10
G = 5
U = 8
HU = U // 2
UA = 4
NBLK = 7
NR = NB // NBLK
AW = D + H
EPS = 1e-5
FAR = 1.0e30
assert FC % SB == 0 and TP % U == 0 and TP >= E // P + NB and NB % NBLK == 0


class Phase:

    def __init__(self, nc):
        self.nc = nc
        self.sems = []
        self.stack = ExitStack()

    def sem(self, name):
        s = self.nc.alloc_semaphore(f"{name}_{self.nc.next_id()}")
        self.sems.append(s)
        return s

    def sb(self, name, shape, dt):
        return self.stack.enter_context(self.nc.sbuf_tensor(f"{name}_{self.nc.next_id()}", shape, dt))

    def ps(self, name, shape, dt=F32):
        return self.stack.enter_context(self.nc.psum_tensor(f"{name}_{self.nc.next_id()}", shape, dt))

    def end(self):
        self.nc.clear_and_free_semaphores(self.sems)
        self.nc.all_engine_barrier()
        self.stack.close()


class Chain:

    def __init__(self, eng, sem):
        self.eng, self.sem, self.n, self.base = eng, sem, 0, 0

    def __call__(self, ins):
        ins.then_inc(self.sem, 1)
        self.n += 1
        self.eng.wait_ge(self.sem, self.base + self.n)

    def round(self, i, steps):
        self.base, self.n = i * steps, 0


def bc(ap, axis, n):
    return ap.unsqueeze(axis).to_broadcast([*ap.shape[:axis], n, *ap.shape[axis:]])


def constants(nc, k):
    ph = Phase(nc)
    made = ph.sem("made")
    block = nc.Block()
    with block as block:
        @block.gpsimd
        def _(pool):
            pool.memset(k.ident[:, :], 0.0).then_inc(made, 1)
            pool.memset(k.ones[:, :], 1.0).then_inc(made, 1)
            pool.memset(k.tri[:, :], 1.0).then_inc(made, 1)
            pool.memset(k.zero_b[:, :], 0.0).then_inc(made, 1)
            pool.iota(k.lanes_i[:, :], [[1, P]], base=0, channel_multiplier=0).then_inc(made, 1)
            pool.iota(k.tiles_i[:, :], [[1, TP]], base=0, channel_multiplier=0).then_inc(made, 1)
            pool.wait_ge(made, 6)
            pool.affine_select(out=k.ident[:, :], in_=k.ident[:, :], compare_op=ALU.not_equal, fill=1.0,
                               base=0, pattern=[[-1, P]], channel_multiplier=1).then_inc(made, 1)
            pool.affine_select(out=k.tri[:, :], in_=k.tri[:, :], compare_op=ALU.is_gt, fill=0.0,
                               base=0, pattern=[[1, P]], channel_multiplier=-1).then_inc(made, 1)
            pool.wait_ge(made, 8)

        @block.vector
        def _(dve):
            dve.wait_ge(made, 8)
            dve.tensor_copy(k.lanes[:, :], k.lanes_i[:, :])
            dve.tensor_copy(k.lanes_b[:, :], k.lanes_i[:, :])
            dve.tensor_copy(k.tiles[:, :], k.tiles_i[:, :])
    ph.end()


def group_edges(nc, k, src, dst, ea128, ea32, x):
    ph = Phase(nc)
    sb = ph.sb
    raw = [sb("raw_src", [P, COLS], I32), sb("raw_dst", [P, COLS], I32)]
    lo = [sb("lo_src", [P, COLS], F32), sb("lo_dst", [P, COLS], F32)]
    hi = [sb("hi_src", [P, COLS], F32), sb("hi_dst", [P, COLS], F32)]
    slot = [sb("slot_src", [P, COLS], I32), sb("slot_dst", [P, COLS], I32)]
    ti = sb("ti", [P, COLS], I32)
    hit = sb("hit", [P, COLS], BF16)
    run = sb("run", [P, COLS], F32)
    pos = sb("pos", [P, COLS], F32)
    hist = sb("hist", [P, NB], F32)
    cnt = sb("cnt", [P, NB], F32)
    cnt_i = sb("cnt_i", [P, NB], I32)
    tls = sb("tls", [P, NB], F32)
    tend = sb("tend", [P, NB], F32)
    base = sb("base", [P, NB], F32)
    ecol = sb("ecol", [P, 1], F32)
    past = sb("past", [P, TP], F32)
    tb_f = sb("tb_f", [1, TP], F32)
    W = [D + 2, DE + 2]
    table = [k.by_src, k.by_dst]
    data = [ea128, ea32]
    pay = [sb("pay_src", [P, SB, W[0]], F32), sb("pay_dst", [P, SB, W[1]], F32)]
    stage = [sb("stage_src", [P, SB], I32), sb("stage_dst", [P, SB], I32)]
    FR = 40
    fill = [sb("fill_src", [P, FR, W[0]], F32), None]
    fill[1] = fill[0][:, :, :].rearrange("p a b -> p (a b)")[:, 0:FR * W[1]].rearrange("p (a b) -> p a b", a=FR)
    fill[0] = fill[0][:, :, :]
    ohl = sb("ohl", [P, 2, G, P], BF16)
    ohh = sb("ohh", [P, 2, G, NB], BF16)
    zb = sb("zb", [P, P], BF16)
    tot_ps, pre_ps, tb_ps = ph.ps("tot", [P, NB]), ph.ps("pre", [P, NB]), ph.ps("tb", [1, 4, 512])
    deg_ps = ph.ps("deg", [P, NB])

    keys_in, fill_set, filled = ph.sem("keys_in"), ph.sem("fill_set"), ph.sem("filled")
    filled2, raw_set, fill2_set = ph.sem("filled2"), ph.sem("raw_set"), ph.sem("fill2_set")
    x_out = ph.sem("x_out")
    chain, hist_ready, sums_ready = ph.sem("chain"), ph.sem("hist_ready"), ph.sem("sums_ready")
    past_ready, tb_ready, slots_ready = ph.sem("past_ready"), ph.sem("tb_ready"), ph.sem("slots_ready")
    pay_in = [[ph.sem(f"pay_in{s}{g}") for g in range(2)] for s in range(2)]
    cols_set = [[ph.sem(f"cols_set{s}{g}") for g in range(2)] for s in range(2)]
    scattered = [[ph.sem(f"scattered{s}{g}") for g in range(2)] for s in range(2)]
    settled, settled_dve = ph.sem("settled"), ph.sem("settled_dve")
    oh_ready, oh_used, deg_ready = ph.sem("oh_ready"), ph.sem("oh_used"), ph.sem("deg_ready")

    with nc.Block() as block:
        @block.sync
        def _(sp):
            sp.wait_ge(raw_set, 2)
            for s, key in enumerate((src, dst)):
                sp.dma_start(raw[s][:, 0:FC], key[0:FC * P].rearrange("(p c) -> p c", p=P)).then_inc(keys_in, 16)
                sp.dma_start(raw[s][0:REST, FC:COLS],
                             key[FC * P:E].rearrange("(p c) -> p c", c=1)).then_inc(keys_in, 16)
            sp.wait_ge(fill_set, 2)
            sp.dma_start(k.x_pad[0:N, :], x).then_inc(x_out, 16)
            sp.dma_start(k.x_pad[N:NP, :], fill[0][0:NP - N, 0, 0:D]).then_inc(x_out, 16)
            sp.wait_ge(x_out, 32)
            for s in range(2):
                rows = data[s][0:FC * P, :].rearrange("(p c) w -> p c w", p=P)
                w = W[s] - 2
                with sp.Fori(0, FC // SB) as i:
                    for g in range(2):
                        sp.wait_ge(scattered[s][g], i * (16 * G))
                        sp.dma_start(pay[s][:, g * G:(g + 1) * G, 0:w],
                                     rows[:, ds(i * SB + g * G, G), :]).then_inc(pay_in[s][g], 16)
                sp.wait_ge(scattered[s][0], FC // 2 * 16)
                sp.dma_start(pay[s][0:REST, 0, 0:w], data[s][FC * P:E, :]).then_inc(pay_in[s][0], 16)

        @block.scalar
        def _(act):
            act.wait_ge(fill_set, 2)
            for c in range(TP // FR):
                act.dma_start(table[0].rearrange("(p r) w -> p r w", p=P)[:, c * FR:(c + 1) * FR, :],
                              fill[0]).then_inc(filled, 16)
            act.wait_ge(filled, 16 * (TP // FR))
            act.nop().then_inc(fill2_set, 1)
            act.wait_ge(fill2_set, 3)
            for c in range(TP // FR):
                act.dma_start(table[1].rearrange("(p r) w -> p r w", p=P)[:, c * FR:(c + 1) * FR, :],
                              fill[1]).then_inc(filled2, 16)
            for s in range(2):
                act.wait_ge(slots_ready, s + 1)
                with act.Fori(0, FC // SB) as i:
                    for g in range(2):
                        c = ds(i * SB + g * G, G)
                        b = slice(g * G, (g + 1) * G)
                        act.wait_ge(scattered[s][g], i * (16 * G))
                        act.copy(stage[s][:, b], slot[s][:, c])
                        act.copy(pay[s][:, b, W[s] - 2], lo[s][:, c])
                        act.copy(pay[s][:, b, W[s] - 1].bitcast(I32), raw[1 - s][:, c]).then_inc(cols_set[s][g], 1)
                act.wait_ge(scattered[s][0], FC // 2 * 16)
                act.copy(stage[s][:, 0:1], slot[s][:, FC:COLS])
                act.copy(pay[s][:, 0, W[s] - 2:W[s] - 1], lo[s][:, FC:COLS])
                act.copy(pay[s][:, 0, W[s] - 1:W[s]].bitcast(I32), raw[1 - s][:, FC:COLS]).then_inc(cols_set[s][0], 1)

        @block.gpsimd
        def _(pool):
            pool.memset(raw[0][:, FC:COLS], -1).then_inc(raw_set, 1)
            pool.memset(raw[1][:, FC:COLS], -1).then_inc(raw_set, 1)
            pool.memset(fill[0], 0.0).then_inc(chain_pool := ph.sem("chain_pool"), 1)
            pool.wait_ge(chain_pool, 1)
            pool.memset(fill[0][:, :, W[0] - 2:W[0] - 1], -1.0).then_inc(fill_set, 2)
            pool.wait_ge(fill2_set, 1)
            pool.wait_ge(x_out, 32)
            pool.memset(fill[1], 0.0).then_inc(fill2_set, 1)
            pool.wait_ge(fill2_set, 2)
            pool.memset(fill[1][:, :, W[1] - 2:W[1] - 1], -1.0).then_inc(fill2_set, 1)

            def put(s, j, rows=P):
                pool.indirect_dma_start(
                    out=table[s], out_offset=bass.IndirectOffsetOnAxis(ap=stage[s][0:rows, j:j + 1], axis=0),
                    in_=pay[s][0:rows, j, :], in_offset=None).then_inc(scattered[s][j // G], 16)

            for s in range(2):
                with pool.Fori(0, FC // SB) as i:
                    for g in range(2):
                        pool.wait_ge(cols_set[s][g], i + 1)
                        pool.wait_ge(pay_in[s][g], i * 16 + 16)
                        pool.wait_ge([filled, filled2][s], 16 * (TP // FR))
                        pool.sem_inc(settled, 1)
                        for j in range(g * G, (g + 1) * G):
                            put(s, j)
                pool.wait_ge(cols_set[s][0], FC // SB + 1)
                pool.wait_ge(pay_in[s][0], FC // SB * 16 + 16)
                put(s, 0, REST)
                pool.wait_ge(scattered[s][0], FC // 2 * 16 + 16)
                pool.wait_ge(scattered[s][1], FC // 2 * 16)

        @block.vector
        def _(dve):
            link = Chain(dve, chain)
            dve.wait_ge(keys_in, 64)
            for s in range(2):
                link(dve.tensor_scalar(ti[:, :], raw[s][:, :], ROW_BITS, None, ALU.arith_shift_right))
                link(dve.tensor_copy(hi[s][:, :], ti[:, :]))
                link(dve.tensor_scalar(ti[:, :], raw[s][:, :], P - 1, None, ALU.bitwise_and))
                link(dve.tensor_copy(lo[s][:, :], ti[:, :]))
            for s in range(2):
                for_hist = link.n
                with dve.Fori(0, NB) as b:
                    link.base = b
                    link(dve.tensor_scalar(hit[:, :], hi[s][:, :], k.lanes[:, ds(b, 1)], 0.0,
                                           ALU.is_equal, ALU.add, accum_out=hist[:, ds(b, 1)]))
                link.base, link.n = 0, for_hist + NB
                dve.wait_ge(chain, link.n)
                dve.nop().then_inc(hist_ready, 1)
                dve.wait_ge(sums_ready, s + 1)
                link(dve.tensor_scalar(cnt_i[:, :], tot_ps[:, :], float(P - 1), None, ALU.add))
                link(dve.tensor_scalar(cnt_i[:, :], cnt_i[:, :], ROW_BITS, None, ALU.arith_shift_right))
                link(dve.tensor_copy(tls[:, :], cnt_i[:, :]))
                link(dve.memset(cnt[:, :], 0.0))
                link(dve.tensor_tensor_scan(tend[:, :], tls[:, :], cnt[:, :], 0.0, ALU.add, ALU.max))
                link(dve.tensor_tensor(tls[:, :], tend[:, :], tls[:, :], ALU.subtract))
                link(dve.scalar_tensor_tensor(base[:, :], tls[:, :], float(P), pre_ps[:, :], ALU.mult, ALU.add))
                link(dve.tensor_tensor(cnt[:, :], tend[:, :], k.ident[:, 0:NB], ALU.mult))
                link(dve.tensor_reduce(ecol[:, :], cnt[:, :], AX, ALU.add))
                dve.tensor_scalar(past[:, :], k.tiles[:, :], ecol[:, 0:1], None, ALU.is_ge).then_inc(past_ready, 1)
                dve.wait_ge(tb_ready, s + 1)
                link(dve.tensor_scalar(tb_f[:, :].rearrange("a (b c) -> a b c", b=4), tb_ps[:, :, 0:TP // 4],
                                       float(NB - 1), None, ALU.min))
                link(dve.tensor_copy(k.tile_block[s][:, :], tb_f[:, :]))
                link(dve.memset(pos[:, :], 0.0))
                for_scan = link.n
                with dve.Fori(0, NB) as b:
                    link.base = b * 3
                    link(dve.tensor_scalar(hit[:, :], hi[s][:, :], k.lanes[:, ds(b, 1)], None, ALU.is_equal))
                    link(dve.tensor_tensor_scan(run[:, :], hit[:, :], hit[:, :], base[:, ds(b, 1)], ALU.add, ALU.max))
                    dve.sem_inc(settled_dve, 1)
                    link(dve.copy_predicated(pos[:, :], hit[:, :].bitcast(I16), run[:, :]))
                link.base, link.n = 0, for_scan + NB * 3
                dve.wait_ge(chain, link.n)
                dve.tensor_scalar(slot[s][:, :], pos[:, :], -1.0, None, ALU.add).then_inc(slots_ready, 1)
                dve.wait_ge(slots_ready, s + 1)
            with dve.Fori(0, FC // SB) as i:
                for g in range(2):
                    dve.wait_ge(oh_used, i * 2 + g + 1)
                    for j in range(G):
                        c = i * SB + g * G + j
                        dve.tensor_scalar(ohl[:, g, j, :], k.lanes_b[:, :], lo[0][:, ds(c, 1)], None, ALU.is_equal)
                        ins = dve.tensor_scalar(ohh[:, g, j, :], k.lanes_b[:, 0:NB], hi[0][:, ds(c, 1)], None,
                                                ALU.is_equal)
                    ins.then_inc(oh_ready, 1)
            dve.wait_ge(oh_used, FC // G + 1)
            dve.tensor_scalar(ohl[:, 0, 0, :], k.lanes_b[:, :], lo[0][:, FC:COLS], None, ALU.is_equal)
            dve.tensor_scalar(ohh[:, 0, 0, :], k.lanes_b[:, 0:NB], hi[0][:, FC:COLS], None,
                              ALU.is_equal).then_inc(oh_ready, 1)
            dve.wait_ge(deg_ready, 1)
            link(dve.tensor_scalar(cnt[:, :], deg_ps[:, :], 1.0, 1.0, ALU.add, ALU.max))
            link(dve.reciprocal(k.dis2[:, :], cnt[:, :]))

        @block.tensor
        def _(pe):
            for s in range(2):
                pe.wait_ge(hist_ready, s + 1)
                pe.matmul(tot_ps[:, :], k.ones[:, :], hist[:, :], start=True, stop=True)
                pe.matmul(pre_ps[:, :], k.tri[:, :], hist[:, :], start=True, stop=True).then_inc(sums_ready, 1)
                pe.wait_ge(past_ready, s + 1)
                for c in range(4):
                    ins = pe.matmul(tb_ps[:, c, 0:TP // 4], k.ones[0:NB, 0:1],
                                    past[0:NB, c * (TP // 4):(c + 1) * (TP // 4)], start=True, stop=True)
                ins.then_inc(tb_ready, 1)
            pe.wait_ge(fill_set, 2)
            pe.matmul(deg_ps[:, :], k.zero_b[:, :], k.lanes_b[:, 0:NB], start=True, stop=False,
                      skip_group_check=True)
            pe.sem_inc(oh_used, 2)
            with pe.Fori(0, FC // SB) as i:
                for g in range(2):
                    pe.wait_ge(oh_ready, i * 2 + g + 1)
                    for j in range(G):
                        ins = pe.matmul(deg_ps[:, :], ohl[:, g, j, :], ohh[:, g, j, :], start=False, stop=False,
                                        skip_group_check=True)
                    ins.then_inc(oh_used, 1)
            pe.wait_ge(oh_ready, FC // G + 1)
            pe.matmul(deg_ps[:, :], ohl[:, 0, 0, :], ohh[:, 0, 0, :], start=False, stop=True,
                      skip_group_check=True).then_inc(deg_ready, 1)
    ph.end()


def load_weights(nc, k, a, sb):
    k.w_att = sb("w_att", [P, 2 * D + 2 * H], F32)
    k.b_att = sb("b_att", [1, 2 * D + 2 * H], F32)
    k.w_msg = sb("w_msg", [P, 2 * D], F32)
    k.b_msg = sb("b_msg", [1, 2 * D], F32)
    k.w_edge = sb("w_edge", [DE, D], F32)
    k.w_out = sb("w_out", [P, D], F32)
    k.b_out = sb("b_out", [1, D], F32)
    k.w_upd = sb("w_upd", [P, D], F32)
    k.b_upd = sb("b_upd", [1, D], F32)
    k.w_up = sb("w_up", [P, 2, 2 * D], F32)
    k.b_up = sb("b_up", [P, 2], F32)
    k.w_down = sb("w_down", [P, 2, D], F32)
    k.b_down = sb("b_down", [1, D], F32)
    k.scales = sb("scales", [P, 4, D], F32)
    ph = Phase(nc)
    w1, w2, wu = ph.sb("w1", [P, 2 * D + DE], F32), ph.sb("w2", [P, D], F32), ph.sb("wu", [P, D], F32)
    turned = ph.ps("turned", [P, 5, 512])
    loaded, cleared, turned_ready = ph.sem("loaded"), ph.sem("cleared"), ph.sem("turned_ready")
    row = lambda v: v.rearrange("(a d) -> a d", a=1)
    c0, c1, c2 = D, D + H, D + 2 * H
    parts = [
        (k.w_att[:, 0:c0], a["L1_gnn_W_l"]), (k.w_att[:, c0:c1], a["L1_gnn_a2w"]),
        (k.w_att[:, c1:c2], a["L1_gnn_a1w"]), (k.w_att[:, c2:], a["L1_gnn_W_r"]),
        (k.b_att[:, c2:], row(a["L1_gnn_bias"])), (k.b_msg[:, D:], row(a["L2_gnn_b1"])),
        (k.b_out[:, :], row(a["L2_gnn_b2"])), (k.b_upd[:, :], row(a["L2_gnn_bu"])),
        (k.w_up[:, :, :], a["L3_gnn_W1"].rearrange("(h p) m -> p h m", p=P)),
        (k.w_down[:, :, :], a["L3_gnn_W2"].rearrange("(h p) m -> p h m", p=P)),
        (k.b_down[:, :], row(a["L3_gnn_b2"])),
        (w1[:, :], a["L2_gnn_W1"]), (w2[:, :], a["L2_gnn_W2"]), (wu[:, :], a["L2_gnn_Wu"]),
        *[(k.b_up[:, h:h + 1], a["L3_gnn_b1"][h * P:(h + 1) * P].rearrange("(p o) -> p o", o=1)) for h in range(2)],
        *[(k.scales[:, n, :], row(a[v]).to_broadcast([P, D])) for n, v in enumerate(
            ("L2_gnn_gamma", "L2_gnn_beta", "L3_gnn_ln_gamma", "L3_gnn_ln_beta"))],
    ]
    with nc.Block() as block:
        @block.sync
        def _(sp):
            sp.wait_ge(cleared, 2)
            for to, of in parts:
                sp.dma_start(to, of).then_inc(loaded, 16)
            sp.wait_ge(loaded, 16 * len(parts))

        @block.tensor
        def _(pe):
            pe.wait_ge(loaded, 16 * len(parts))
            pe.transpose(turned[:, 0, 0:P], w1[:, 0:D], k.ident[:, :])
            pe.transpose(turned[:, 1, 0:P], w1[:, D:2 * D], k.ident[:, :])
            pe.transpose(turned[0:DE, 2, 0:P], w1[:, 2 * D:], k.ident[:, :])
            pe.transpose(turned[:, 3, 0:P], w2[:, :], k.ident[:, :])
            pe.transpose(turned[:, 4, 0:P], wu[:, :], k.ident[:, :]).then_inc(turned_ready, 1)

        @block.vector
        def _(dve):
            dve.memset(k.b_att[:, 0:c2], 0.0).then_inc(cleared, 1)
            dve.memset(k.b_msg[:, 0:D], 0.0).then_inc(cleared, 1)
            dve.wait_ge(turned_ready, 1)
            for to, n in ((k.w_msg[:, 0:D], 0), (k.w_msg[:, D:], 1), (k.w_edge[:, :], 2), (k.w_out[:, :], 3),
                          (k.w_upd[:, :], 4)):
                dve.tensor_copy(to, turned[0:to.shape[0], n, 0:P])
    ph.end()


def blocks_of(table):
    return table.rearrange("(b p) d -> p b d", p=P)


def scale_nodes(nc, k, x, scaled):
    ph = Phase(nc)
    xb, gb = ph.sb("xb", [P, 2, NBLK, D], F32), ph.sb("gb", [P, 2, NBLK, D], F32)
    root, dis_ready = ph.sem("root"), ph.sem("dis_ready")
    loaded, stored = [ph.sem("loaded0"), ph.sem("loaded1")], [ph.sem("stored0"), ph.sem("stored1")]
    made = ph.sem("made")
    with nc.Block() as block:
        @block.sync
        def _(sp):
            with sp.Fori(0, NR // 2) as i:
                for r in range(2):
                    sp.wait_ge(stored[r], i * 16)
                    sp.dma_start(xb[:, r], blocks_of(x)[:, ds((i * 2 + r) * NBLK, NBLK), :]).then_inc(loaded[r], 16)

        @block.scalar
        def _(act):
            act.activation(k.dis[:, :], k.dis2[:, :], ACT.Sqrt).then_inc(dis_ready, 1)
            with act.Fori(0, NR // 2) as i:
                for r in range(2):
                    act.wait_ge(made, i * 2 + r + 1)
                    act.dma_start(blocks_of(scaled)[:, ds((i * 2 + r) * NBLK, NBLK), :], gb[:, r]).then_inc(stored[r], 16)
            for r in range(2):
                act.wait_ge(stored[r], NR // 2 * 16)

        @block.vector
        def _(dve):
            dve.wait_ge(dis_ready, 1)
            with dve.Fori(0, NR // 2) as i:
                for r in range(2):
                    dve.wait_ge(loaded[r], i * 16 + 16)
                    dve.wait_ge(stored[r], i * 16)
                    for j in range(NBLK):
                        ins = dve.tensor_scalar(gb[:, r, j], xb[:, r, j], k.dis[:, ds((i * 2 + r) * NBLK + j, 1)],
                                                None, ALU.mult)
                    ins.then_inc(made, 1)
    ph.end()


def hop(nc, k, table, attributes, sums, nxt):
    ph = Phase(nc)
    W = 2 * D if attributes is not None else D
    rows = ph.sb("rows", [P, U, W], F32)
    onehot = ph.sb("onehot", [P, U, P], F32)
    stage = ph.sb("stage", [P, U], I32)
    own, gb = ph.sb("own", [P, 2, NBLK, D], F32), ph.sb("gb", [P, 2, NBLK, D], F32)
    part = [ph.ps(f"part{j}", [P, 512]) for j in range(4)]
    zeroed, staged, chain = ph.sem("zeroed"), ph.sem("staged"), ph.sem("chain")
    gathered = [ph.sem(f"gathered{u}") for u in range(U)]
    attr_in = [ph.sem("attr_in0"), ph.sem("attr_in1")]
    hot, multiplied, added = ph.sem("hot"), ph.sem("multiplied"), ph.sem("added")
    own_in, stored = [ph.sem("own_in0"), ph.sem("own_in1")], [ph.sem("stored0"), ph.sem("stored1")]
    made, settled, sums_out = ph.sem("made"), ph.sem("settled"), ph.sem("sums_out")

    with nc.Block() as block:
        @block.sync
        def _(sp):
            if attributes is not None:
                with sp.Fori(0, TP // U) as i:
                    for h in range(2):
                        sp.wait_ge(multiplied, i * U + h * HU + HU)
                        sp.dma_start(rows[:, h * HU:(h + 1) * HU, D:2 * D],
                                     attributes.rearrange("(t p) w -> p t w", p=P)[:, ds(i * U + h * HU, HU), 0:D])\
                          .then_inc(attr_in[h], 16)
                sp.wait_ge(added, 4 + TP)
                sp.dma_start(blocks_of(sums), k.acc2[:, :, :]).then_inc(sums_out, 16)
            with sp.Fori(0, NR // 2) as i:
                for r in range(2):
                    if nxt is not None:
                        sp.wait_ge(stored[r], i * 16)
                        sp.dma_start(own[:, r], blocks_of(table)[:, ds((i * 2 + r) * NBLK, NBLK), :])\
                          .then_inc(own_in[r], 16)
            if attributes is not None:
                sp.wait_ge(sums_out, 16)

        @block.scalar
        def _(act):
            with act.Fori(0, TP // U) as i:
                for h in range(2):
                    for u in range(h * HU, (h + 1) * HU):
                        act.wait_ge(gathered[u], i * 16)
                    act.copy(stage[:, h * HU:(h + 1) * HU], k.nodes[0][:, ds(i * U + h * HU, HU), 1].bitcast(I32))\
                       .then_inc(staged, 1)
            if nxt is not None:
                with act.Fori(0, NR // 2) as i:
                    for r in range(2):
                        act.wait_ge(made, i * 2 + r + 1)
                        act.dma_start(blocks_of(nxt)[:, ds((i * 2 + r) * NBLK, NBLK), :], gb[:, r])\
                           .then_inc(stored[r], 16)
                for r in range(2):
                    act.wait_ge(stored[r], NR // 2 * 16)

        @block.gpsimd
        def _(pool):
            with pool.Fori(0, TP // U) as i:
                for h in range(2):
                    pool.wait_ge(staged, i * 2 + h + 1)
                    pool.wait_ge(multiplied, i * U + h * HU + HU)
                    pool.sem_inc(settled, 1)
                    for u in range(h * HU, (h + 1) * HU):
                        pool.indirect_dma_start(
                            out=rows[:, u, 0:D], out_offset=None, in_=table,
                            in_offset=bass.IndirectOffsetOnAxis(ap=stage[:, u:u + 1], axis=0)).then_inc(gathered[u], 16)

        @block.tensor
        def _(pe):
            pe.sem_inc(multiplied, U)
            with pe.Fori(0, TP // U) as i:
                for u in range(U):
                    if u % HU == 0 and attributes is not None:
                        pe.wait_ge(attr_in[u // HU], i * 16 + 16)
                    pe.wait_ge(hot, i * U + u + 1)
                    pe.wait_ge(gathered[u], i * 16 + 16)
                    pe.wait_ge(added, i * U + u + 1)
                    pe.matmul(part[u % 4][:, 0:W], onehot[:, u, :], rows[:, u, :], start=True, stop=True)\
                      .then_inc(multiplied, 1)

        @block.vector
        def _(dve):
            dve.memset(k.acc[:, :, :], 0.0).then_inc(zeroed, 1)
            if attributes is not None:
                dve.memset(k.acc2[:, :, :], 0.0).then_inc(zeroed, 1)
            dve.wait_ge(zeroed, 2 if attributes is not None else 1)
            dve.sem_inc(added, 4)
            with dve.Fori(0, TP // U) as i:
                for u in range(U):
                    dve.wait_ge(multiplied, i * U + u + 1)
                    dve.tensor_scalar(onehot[:, u, :], k.lanes[:, :], k.nodes[0][:, ds(i * U + u, 1), 0], None,
                                      ALU.is_equal).then_inc(hot, 1)
                for u in range(U):
                    b = dve.value_load(k.tile_block[0][0:1, ds(i * U + u, 1)], min_val=0, max_val=NB - 1)
                    dve.wait_ge(multiplied, i * U + u + 1 + U)
                    dve.wait_ge(added, i * U + u + 4)
                    if attributes is not None:
                        dve.tensor_tensor(k.acc2[:, ds(b, 1), :], k.acc2[:, ds(b, 1), :],
                                          part[u % 4][:, D:2 * D].unsqueeze(1), ALU.add)
                    dve.tensor_tensor(k.acc[:, ds(b, 1), 0:D], k.acc[:, ds(b, 1), 0:D],
                                      part[u % 4][:, 0:D].unsqueeze(1), ALU.add).then_inc(added, 1)
            dve.wait_ge(added, 4 + TP)
            if nxt is not None:
                with dve.Fori(0, NR // 2) as i:
                    for r in range(2):
                        first = (i * 2 + r) * NBLK
                        dve.wait_ge(own_in[r], i * 16 + 16)
                        dve.wait_ge(stored[r], i * 16)
                        dve.tensor_tensor(own[:, r], own[:, r], k.acc[:, ds(first, NBLK), 0:D], ALU.add)\
                           .then_inc(chain, 1)
                        dve.wait_ge(chain, i * 2 + r + 1)
                        for j in range(NBLK):
                            ins = dve.tensor_scalar(gb[:, r, j], own[:, r, j], k.dis2[:, ds(first + j, 1)], None,
                                                    ALU.mult)
                        ins.then_inc(made, 1)
    ph.end()


def fetch_nodes(nc, k):
    ph = Phase(nc)
    loaded = ph.sem("loaded")
    with nc.Block() as block:
        for s, (eng, table, w) in enumerate(((block.sync, k.by_src, D), (block.scalar, k.by_dst, DE))):
            def fetch(q, s=s, table=table, w=w):
                q.dma_start(k.nodes[s][:, :, :], table.rearrange("(t p) w -> p t w", p=P)[:, :, w:w + 2])\
                 .then_inc(loaded, 16)
                q.wait_ge(loaded, 32)
            eng(fetch)
    ph.end()


class Norm:

    def __init__(self, ph):
        self.stats = ph.sb("stats", [P, NBLK, 6], F32)
        self.mv = ph.sb("mv", [P, NBLK, 2], F32)
        self.std = ph.sb("std", [P, NBLK], F32)
        self.rstd = ph.sb("rstd", [P, NBLK], F32)
        self.settled = ph.sem("settled_stats")
        self.var_ready, self.std_ready = ph.sem("var_ready"), ph.sem("std_ready")

    def root(self, act, nth):
        act.wait_ge(self.var_ready, nth)
        act.activation(self.std[:, :], self.rstd[:, :], ACT.Sqrt).then_inc(self.std_ready, 1)

    def __call__(self, dve, link, y, out, nth):
        for j in range(NBLK):
            ins = dve.bn_stats(self.stats[:, j, :], y[:, j, :])
        link(ins)
        dve.sem_inc(self.settled, 1)
        for j in range(NBLK):
            ins = dve.bn_aggr(self.mv[:, j, :], self.stats[:, j, :])
        link(ins)
        dve.tensor_scalar(self.rstd[:, :], self.mv[:, :, 1], EPS, None, ALU.add).then_inc(self.var_ready, 1)
        dve.wait_ge(self.std_ready, nth)
        link(dve.reciprocal(self.rstd[:, :], self.std[:, :]))
        for j in range(NBLK):
            ins = dve.tensor_scalar(out[:, j, :], y[:, j, :], self.mv[:, j, 0:1], self.rstd[:, j:j + 1],
                                    ALU.subtract, ALU.mult)
        link(ins)


def bank(ps, j, n=P):
    return ps[:, j // 4, (j % 4) * P:(j % 4) * P + n]


def banks(ps):
    return [(slice(0, 4), ps[:, 0, 0:4 * P].rearrange("p (j n) -> p j n", j=4)),
            (slice(4, 7), ps[:, 1, 0:3 * P].rearrange("p (j n) -> p j n", j=3))]


def to_attention(nc, k, table, x, att_table, rest_table):
    ph = Phase(nc)
    norm = Norm(ph)
    WT = 2 * D + 2 * H
    own, xb = ph.sb("own", [P, 2, NBLK, D], F32), ph.sb("xb", [P, 2, NBLK, D], F32)
    xn, xT = ph.sb("xn", [P, NBLK, D], F32), ph.sb("xT", [P, NBLK, D], F32)
    tl, yb = ph.sb("tl", [P, 2, NBLK, AW], F32), ph.sb("yb", [P, 2, NBLK, D], F32)
    turned = ph.ps("turned", [P, 2, 512])
    prod = [ph.ps(f"prod{j}", [P, 512]) for j in range(4)]
    loaded, stored = [ph.sem("loaded0"), ph.sem("loaded1")], [ph.sem("stored0"), ph.sem("stored1")]
    chain, xn_ready, turned_ready = ph.sem("chain"), ph.sem("xn_ready"), ph.sem("turned_ready")
    xT_ready, prod_ready = ph.sem("xT_ready"), ph.sem("prod_ready")
    copied, taken, settled = ph.sem("copied"), ph.sem("taken"), ph.sem("settled")
    with nc.Block() as block:
        @block.sync
        def _(sp):
            with sp.Fori(0, NR // 2) as i:
                for r in range(2):
                    b = ds((i * 2 + r) * NBLK, NBLK)
                    sp.wait_ge(stored[r], i * 32)
                    sp.dma_start(own[:, r], blocks_of(table)[:, b, :]).then_inc(loaded[r], 16)
                    sp.dma_start(xb[:, r], blocks_of(x)[:, b, :]).then_inc(loaded[r], 16)

        @block.gpsimd
        def _(pool):
            with pool.Fori(0, NR // 2) as i:
                for r in range(2):
                    b = ds((i * 2 + r) * NBLK, NBLK)
                    pool.wait_ge(copied, (i * 2 + r + 1) * NBLK)
                    pool.sem_inc(settled, 1)
                    pool.dma_start(blocks_of(att_table)[:, b, :], tl[:, r]).then_inc(stored[r], 16)
                    pool.wait_ge(taken, (i * 2 + r + 1) * NBLK + 4)
                    pool.sem_inc(settled, 1)
                    pool.dma_start(blocks_of(rest_table)[:, b, :], yb[:, r]).then_inc(stored[r], 16)
            for r in range(2):
                pool.wait_ge(stored[r], NR // 2 * 32)

        @block.scalar
        def _(act):
            with act.Fori(0, NR // 2) as i:
                for r in range(2):
                    R = i * 2 + r
                    norm.root(act, R + 1)
                    act.wait_ge(turned_ready, R + 1)
                    act.wait_ge(prod_ready, R * NBLK)
                    for sl, ps in banks(turned):
                        ins = act.copy(xT[:, sl, :], ps)
                    ins.then_inc(xT_ready, 1)
                    act.wait_ge(stored[r], i * 32)
                    for j in range(NBLK):
                        act.wait_ge(prod_ready, R * NBLK + j + 1)
                        act.copy(tl[:, r, j, :], prod[j % 4][:, 0:AW]).then_inc(copied, 1)

        @block.tensor
        def _(pe):
            with pe.Fori(0, NR // 2) as i:
                for r in range(2):
                    R = i * 2 + r
                    pe.wait_ge(xn_ready, R + 1)
                    pe.wait_ge(xT_ready, R)
                    for j in range(NBLK):
                        ins = pe.transpose(bank(turned, j), xn[:, j, :], k.ident[:, :])
                    ins.then_inc(turned_ready, 1)
                    pe.wait_ge(xT_ready, R + 1)
                    for j in range(NBLK):
                        pe.wait_ge(taken, R * NBLK + j + 1)
                        if j >= 4:
                            pe.wait_ge(copied, R * NBLK + j - 3)
                        else:
                            pe.wait_ge(copied, R * NBLK)
                        pe.matmul(prod[j % 4][:, 0:WT], xT[:, j, :], k.w_att[:, :], start=True, stop=False)
                        pe.matmul(prod[j % 4][:, 0:WT], k.ones[0:1, :], k.b_att[:, :], start=False, stop=True)\
                          .then_inc(prod_ready, 1)

        @block.vector
        def _(dve):
            link = Chain(dve, chain)
            dve.sem_inc(taken, 4)
            with dve.Fori(0, NR // 2) as i:
                for r in range(2):
                    R = i * 2 + r
                    first = R * NBLK
                    link.round(R, 6)
                    dve.wait_ge(loaded[r], i * 32 + 32)
                    dve.wait_ge(stored[r], i * 32)
                    link(dve.tensor_tensor(own[:, r], own[:, r], k.acc[:, ds(first, NBLK), 0:D], ALU.add))
                    for j in range(NBLK):
                        ins = dve.scalar_tensor_tensor(xb[:, r, j], own[:, r, j], k.dis[:, ds(first + j, 1)],
                                                       xb[:, r, j], ALU.mult, ALU.add)
                    link(ins)
                    norm(dve, link, xb[:, r], xn, R + 1)
                    dve.nop().then_inc(xn_ready, 1)
                    for j in range(NBLK):
                        dve.wait_ge(copied, R * NBLK + j + 1)
                        dve.sem_inc(norm.settled, 1)
                        dve.tensor_copy(k.a1[:, ds(first + j, 1), :], prod[j % 4][:, D + H:D + 2 * H].unsqueeze(1))
                        dve.tensor_tensor(yb[:, r, j, :], xn[:, j, :], prod[j % 4][:, D + 2 * H:WT], ALU.add)\
                           .then_inc(taken, 1)
    ph.end()



def attention(nc, k, att_table):
    ph = Phase(nc)
    rows = ph.sb("rows", [P, U, AW], F32)
    weighed = ph.sb("weighed", [P, UA, H, HD + 1], F32)
    onehot, turned_sb = ph.sb("onehot", [P, U, P], F32), ph.sb("turned_sb", [P, UA, P], F32)
    mask = ph.sb("mask", [P, UA, P], F32)
    junk = ph.sb("junk", [P, H, P], F32)
    stage = ph.sb("stage", [P, U], I32)
    top = ph.sb("top", [P, UA, H], F32)
    pair = ph.sb("pair", [P, UA, 2, H], F32)
    look = ph.sb("look", [P, UA, 2, H], F32)
    drop = ph.sb("drop", [P, UA, H], F32)
    corr = ph.sb("corr", [P, UA, H], F32)
    score = ph.sb("score", [P, UA, H], F32)
    scaled = ph.sb("scaled", [P, H, HD + 1], F32)
    turned = [ph.ps(f"turned{j}", [P, 512]) for j in range(2)]
    values = [ph.ps(f"values{j}", [P, H, P]) for j in range(2)]
    looked = [ph.ps(f"looked{j}", [P, 512]) for j in range(2)]
    part = [ph.ps(f"part{j}", [P, 512]) for j in range(2)]
    zeroed, staged, chain = ph.sem("zeroed"), ph.sem("staged"), ph.sem("chain")
    gathered = [ph.sem(f"gathered{u}") for u in range(U)]
    used, hot, turned_ready, mask_ready = ph.sem("used"), ph.sem("hot"), ph.sem("turned_ready"), ph.sem("mask_ready")
    values_ready, drop_ready, corr_ready = ph.sem("values_ready"), ph.sem("drop_ready"), ph.sem("corr_ready")
    looked_ready, score_ready, weight_ready = ph.sem("looked_ready"), ph.sem("score_ready"), ph.sem("weight_ready")
    weighed_ready, added, settled = ph.sem("weighed_ready"), ph.sem("added"), ph.sem("settled")
    scaled_ready = ph.sem("scaled_ready")
    STEPS = UA * 8

    with nc.Block() as block:
        @block.scalar
        def _(act):
            with act.Fori(0, TP // U) as i:
                for h in range(2):
                    for u in range(h * HU, (h + 1) * HU):
                        act.wait_ge(gathered[u], i * 16)
                    act.copy(stage[:, h * HU:(h + 1) * HU], k.nodes[0][:, ds(i * U + h * HU, HU), 1].bitcast(I32))\
                       .then_inc(staged, 1)
                    for u in range(h * UA, (h + 1) * UA):
                        n, v = i * U + u, u % UA
                        act.wait_ge(turned_ready, n + 1)
                        act.wait_ge(used, n + 1 + U - UA)
                        act.copy(turned_sb[:, v, :], turned[v % 2][:, 0:P])
                        act.activation(mask[:, v, :], turned[v % 2][:, 0:P], ACT.Copy, scale=FAR, bias=-FAR)\
                           .then_inc(mask_ready, 1)
                    for u in range(h * UA, (h + 1) * UA):
                        n, v = i * U + u, u % UA
                        act.wait_ge(drop_ready, n + 3)
                        act.activation(corr[:, v, :], drop[:, v, :], ACT.Exp).then_inc(corr_ready, 1)
                    for u in range(h * UA, (h + 1) * UA):
                        n, v = i * U + u, u % UA
                        act.wait_ge(score_ready, n + 3)
                        act.activation(weighed[:, v, :, HD], score[:, v, :], ACT.Exp).then_inc(weight_ready, 1)

        @block.gpsimd
        def _(pool):
            with pool.Fori(0, TP // U) as i:
                for h in range(2):
                    pool.wait_ge(staged, i * 2 + h + 1)
                    pool.wait_ge(used, i * U + h * HU + HU)
                    pool.sem_inc(settled, 1)
                    for u in range(h * HU, (h + 1) * HU):
                        pool.indirect_dma_start(
                            out=rows[:, u, :], out_offset=None, in_=att_table,
                            in_offset=bass.IndirectOffsetOnAxis(ap=stage[:, u:u + 1], axis=0)).then_inc(gathered[u], 16)

        @block.tensor
        def _(pe):
            pe.sem_inc(used, U)
            with pe.Fori(0, TP // U) as i:
                for h in range(2):
                    for u in range(h * UA, (h + 1) * UA):
                        n, v = i * U + u, u % UA
                        pe.wait_ge(hot, n + 1)
                        pe.wait_ge(mask_ready, n + 1)
                        pe.transpose(turned[v % 2][:, 0:P], onehot[:, u, :], k.ident[:, :]).then_inc(turned_ready, 1)
                        pe.wait_ge(gathered[u], i * 16 + 16)
                        pe.wait_ge(drop_ready, n + 1)
                        for q in range(H):
                            ins = pe.matmul(values[v % 2][:, q, :], rows[:, u, D + q:D + q + 1].to_broadcast([P, P]),
                                            k.ident[:, :], start=True, stop=True)
                        ins.then_inc(values_ready, 1)
                    for u in range(h * UA, (h + 1) * UA):
                        n, v = i * U + u, u % UA
                        pe.wait_ge(drop_ready, n + 3)
                        pe.wait_ge(score_ready, n + 1)
                        pe.matmul(looked[v % 2][:, 0:2 * H], turned_sb[:, v, :],
                                  look[:, v, :, :].rearrange("p a b -> p (a b)"), start=True, stop=True)\
                          .then_inc(looked_ready, 1)
                    for u in range(h * UA, (h + 1) * UA):
                        n, v = i * U + u, u % UA
                        pe.wait_ge(weighed_ready, n + 1)
                        pe.wait_ge(added, n + 1)
                        pe.matmul(part[v % 2][:, 0:AW], onehot[:, u, :],
                                  weighed[:, v, :, :].rearrange("p a b -> p (a b)"), start=True, stop=True)\
                          .then_inc(used, 1)

        @block.vector
        def _(dve):
            link = Chain(dve, chain)
            dve.memset(k.acc[:, :, :], 0.0).then_inc(zeroed, 1)
            dve.memset(k.top[:, :, :], -FAR).then_inc(zeroed, 1)
            dve.wait_ge(zeroed, 2)
            for s in (mask_ready, drop_ready, score_ready, added):
                dve.sem_inc(s, 2)
            with dve.Fori(0, TP // U) as i:
                for h in range(2):
                    link.round(i * 2 + h, STEPS)
                    at = []
                    for u in range(h * UA, (h + 1) * UA):
                        n, v = i * U + u, u % UA
                        dve.wait_ge(used, n + 1)
                        dve.tensor_scalar(onehot[:, u, :], k.lanes[:, :], k.nodes[0][:, ds(n, 1), 0], None,
                                          ALU.is_equal).then_inc(hot, 1)
                    for u in range(h * UA, (h + 1) * UA):
                        n, v = i * U + u, u % UA
                        b = dve.value_load(k.tile_block[0][0:1, ds(n, 1)], min_val=0, max_val=NB - 1)
                        at.append(b)
                        dve.wait_ge(mask_ready, n + 3)
                        dve.wait_ge(values_ready, n + 1)
                        dve.sem_inc(settled, 1)
                        for q in range(H):
                            ins = dve.tensor_tensor_reduce(junk[:, q, :], values[v % 2][:, q, :], mask[:, v, :], 1.0,
                                                           -FAR, ALU.add, ALU.max, top[:, v, q:q + 1])
                        dve.tensor_copy(pair[:, v, 0:1, :], k.top[:, ds(b, 1), :])
                        dve.tensor_copy(look[:, v, 0:1, :], k.a1[:, ds(b, 1), :])
                        link(ins)
                        dve.tensor_tensor(pair[:, v, 1:2, :], k.top[:, ds(b, 1), :], top[:, v:v + 1, :], ALU.max)
                        link(dve.tensor_tensor(k.top[:, ds(b, 1), :], k.top[:, ds(b, 1), :], top[:, v:v + 1, :], ALU.max))
                        link(dve.tensor_tensor(pair[:, v, :, :], pair[:, v, :, :],
                                               k.a1[:, ds(b, 1), :].to_broadcast([P, 2, H]), ALU.add))
                        link(dve.scalar_tensor_tensor(pair[:, v, :, :], pair[:, v, :, :], 0.2, pair[:, v, :, :],
                                                      ALU.mult, ALU.max))
                        link(dve.tensor_copy(look[:, v, 1, :], pair[:, v, 1, :]))
                        dve.tensor_tensor(drop[:, v, :], pair[:, v, 0, :], pair[:, v, 1, :], ALU.subtract)\
                           .then_inc(drop_ready, 1)
                    for u in range(h * UA, (h + 1) * UA):
                        n, v = i * U + u, u % UA
                        dve.wait_ge(looked_ready, n + 1)
                        link(dve.tensor_tensor(score[:, v, :], looked[v % 2][:, 0:H], rows[:, u, D:AW], ALU.add))
                        link(dve.scalar_tensor_tensor(score[:, v, :], score[:, v, :], 0.2, score[:, v, :],
                                                      ALU.mult, ALU.max))
                        link(dve.tensor_tensor(score[:, v, :], score[:, v, :], looked[v % 2][:, H:2 * H], ALU.subtract))
                        dve.tensor_scalar(score[:, v, :], score[:, v, :], 0.0, None, ALU.min).then_inc(score_ready, 1)
                    for u in range(h * UA, (h + 1) * UA):
                        n, v = i * U + u, u % UA
                        dve.wait_ge(weight_ready, n + 1)
                        dve.tensor_tensor(weighed[:, v, :, 0:HD], rows[:, u, 0:D].rearrange("p (a b) -> p a b", a=H),
                                          weighed[:, v, :, HD:HD + 1].to_broadcast([P, H, HD]), ALU.mult)\
                           .then_inc(weighed_ready, 1)
                    for u in range(h * UA, (h + 1) * UA):
                        n, v = i * U + u, u % UA
                        own = k.acc[:, ds(at[v], 1), :].rearrange("p o (a b) -> p (o a) b", a=H)
                        dve.wait_ge(corr_ready, n + 1)
                        dve.wait_ge(added, n + 2)
                        dve.tensor_tensor(scaled[:, :, :], own, corr[:, v, :].unsqueeze(2).to_broadcast([P, H, HD + 1]),
                                          ALU.mult).then_inc(scaled_ready, 1)
                        dve.wait_ge(scaled_ready, n + 1)
                        dve.wait_ge(used, n + 1 + U)
                        dve.tensor_tensor(own, scaled[:, :, :],
                                          part[v % 2][:, 0:AW].rearrange("p (a b) -> p a b", a=H), ALU.add)\
                           .then_inc(added, 1)
    ph.end()


def to_messages(nc, k, rest_table, x2_table, p_table):
    ph = Phase(nc)
    norm = Norm(ph)
    xb = ph.sb("xb", [P, 2, NBLK, D], F32)
    msg, inv = ph.sb("msg", [P, NBLK, D], F32), ph.sb("inv", [P, NBLK, H], F32)
    xn, xT = ph.sb("xn", [P, 2, NBLK, D], F32), ph.sb("xT", [P, NBLK, D], F32)
    pb = ph.sb("pb", [P, 2, NBLK, D], F32)
    turned = ph.ps("turned", [P, 2, 512])
    prod = [ph.ps(f"prod{j}", [P, 512]) for j in range(4)]
    loaded, stored = [ph.sem("loaded0"), ph.sem("loaded1")], [ph.sem("stored0"), ph.sem("stored1")]
    chain, xn_ready, turned_ready = ph.sem("chain"), ph.sem("xn_ready"), ph.sem("turned_ready")
    xT_ready, prod_ready, settled = ph.sem("xT_ready"), ph.sem("prod_ready"), ph.sem("settled")
    copied, taken = ph.sem("copied"), ph.sem("taken")
    with nc.Block() as block:
        @block.sync
        def _(sp):
            with sp.Fori(0, NR // 2) as i:
                for r in range(2):
                    sp.wait_ge(stored[r], i * 32)
                    sp.dma_start(xb[:, r], blocks_of(rest_table)[:, ds((i * 2 + r) * NBLK, NBLK), :])\
                      .then_inc(loaded[r], 16)

        @block.gpsimd
        def _(pool):
            with pool.Fori(0, NR // 2) as i:
                for r in range(2):
                    b = ds((i * 2 + r) * NBLK, NBLK)
                    pool.wait_ge(xn_ready, i * 2 + r + 1)
                    pool.sem_inc(settled, 1)
                    pool.dma_start(blocks_of(x2_table)[:, b, :], xn[:, r]).then_inc(stored[r], 16)
                    pool.wait_ge(copied, (i * 2 + r + 1) * NBLK)
                    pool.sem_inc(settled, 1)
                    pool.dma_start(blocks_of(p_table)[:, b, :], pb[:, r]).then_inc(stored[r], 16)
            for r in range(2):
                pool.wait_ge(stored[r], NR // 2 * 32)

        @block.scalar
        def _(act):
            with act.Fori(0, NR // 2) as i:
                for r in range(2):
                    R = i * 2 + r
                    norm.root(act, R + 1)
                    act.wait_ge(turned_ready, R + 1)
                    act.wait_ge(prod_ready, R * NBLK)
                    for sl, ps in banks(turned):
                        ins = act.copy(xT[:, sl, :], ps)
                    ins.then_inc(xT_ready, 1)
                    act.wait_ge(stored[r], i * 32)
                    for j in range(NBLK):
                        act.wait_ge(prod_ready, R * NBLK + j + 1)
                        act.copy(pb[:, r, j, :], prod[j % 4][:, 0:D]).then_inc(copied, 1)

        @block.tensor
        def _(pe):
            with pe.Fori(0, NR // 2) as i:
                for r in range(2):
                    R = i * 2 + r
                    pe.wait_ge(xn_ready, R + 1)
                    pe.wait_ge(xT_ready, R)
                    for j in range(NBLK):
                        ins = pe.transpose(bank(turned, j), xn[:, r, j, :], k.ident[:, :])
                    ins.then_inc(turned_ready, 1)
                    pe.wait_ge(xT_ready, R + 1)
                    for j in range(NBLK):
                        pe.wait_ge(taken, R * NBLK + j + 1)
                        pe.wait_ge(copied, R * NBLK + j - 3 if j >= 4 else R * NBLK)
                        pe.matmul(prod[j % 4][:, 0:2 * D], xT[:, j, :], k.w_msg[:, :], start=True, stop=False)
                        pe.matmul(prod[j % 4][:, 0:2 * D], k.ones[0:1, :], k.b_msg[:, :], start=False, stop=True)\
                          .then_inc(prod_ready, 1)

        @block.vector
        def _(dve):
            link = Chain(dve, chain)
            dve.sem_inc(taken, 4)
            with dve.Fori(0, NR // 2) as i:
                for r in range(2):
                    R = i * 2 + r
                    first = R * NBLK
                    sums = k.acc[:, ds(first, NBLK), :].rearrange("p n (a b) -> p n a b", a=H)
                    link.round(R, 8)
                    dve.wait_ge(loaded[r], i * 16 + 16)
                    dve.wait_ge(stored[r], i * 32)
                    link(dve.tensor_scalar(inv[:, :, :], sums[:, :, :, HD], 0.5, None, ALU.max))
                    link(dve.reciprocal(inv[:, :, :], inv[:, :, :]))
                    for j in range(NBLK):
                        ins = dve.tensor_tensor(msg[:, j, :].rearrange("p (a b) -> p a b", a=H),
                                                k.acc[:, ds(first + j, 1), :].rearrange("p o (a b) -> p (o a) b", a=H)[:, :, 0:HD],
                                                inv[:, j, :].unsqueeze(2).to_broadcast([P, H, HD]), ALU.mult)
                    link(ins)
                    link(dve.tensor_tensor(xb[:, r], xb[:, r], msg[:, :, :], ALU.add))
                    norm(dve, link, xb[:, r], xn[:, r], R + 1)
                    dve.nop().then_inc(xn_ready, 1)
                    for j in range(NBLK):
                        dve.wait_ge(copied, R * NBLK + j + 1)
                        dve.sem_inc(norm.settled, 1)
                        dve.tensor_copy(k.acc2[:, ds(first + j, 1), :], prod[j % 4][:, D:2 * D].unsqueeze(1))\
                           .then_inc(taken, 1)
    ph.end()


def messages(nc, k, p_table):
    ph = Phase(nc)
    rows = ph.sb("rows", [P, U, D], F32)
    attr, attr_t = ph.sb("attr", [P, U, DE], F32), ph.sb("attr_t", [DE, UA, P], F32)
    onehot, turned_sb = ph.sb("onehot", [P, U, P], F32), ph.sb("turned_sb", [P, UA, P], F32)
    pre, hid = ph.sb("pre", [P, UA, D], F32), ph.sb("hid", [P, UA, D + 1], F32)
    stage = ph.sb("stage", [P, U], I32)
    turned = [ph.ps(f"turned{j}", [P, 512]) for j in range(2)]
    local = [ph.ps(f"local{j}", [P, 512]) for j in range(2)]
    part = [ph.ps(f"part{j}", [P, 512]) for j in range(2)]
    zeroed, staged, settled = ph.sem("zeroed"), ph.sem("staged"), ph.sem("settled")
    gathered = [ph.sem(f"gathered{u}") for u in range(U)]
    attr_in = [ph.sem("attr_in0"), ph.sem("attr_in1")]
    used, hot, turned_ready = ph.sem("used"), ph.sem("hot"), ph.sem("turned_ready")
    copied, local_ready, pre_ready = ph.sem("copied"), ph.sem("local_ready"), ph.sem("pre_ready")
    hid_ready, added = ph.sem("hid_ready"), ph.sem("added")

    with nc.Block() as block:
        @block.sync
        def _(sp):
            with sp.Fori(0, TP // U) as i:
                for h in range(2):
                    sp.wait_ge(used, i * U + h * HU + HU)
                    sp.dma_start(attr[:, h * HU:(h + 1) * HU, :],
                                 k.by_dst.rearrange("(t p) w -> p t w", p=P)[:, ds(i * U + h * HU, HU), 0:DE])\
                      .then_inc(attr_in[h], 16)

        @block.scalar
        def _(act):
            act.wait_ge(zeroed, 2)
            with act.Fori(0, TP // U) as i:
                for h in range(2):
                    for u in range(h * HU, (h + 1) * HU):
                        act.wait_ge(gathered[u], i * 16)
                    act.copy(stage[:, h * HU:(h + 1) * HU], k.nodes[1][:, ds(i * U + h * HU, HU), 1].bitcast(I32))\
                       .then_inc(staged, 1)
                    for u in range(h * UA, (h + 1) * UA):
                        n, v = i * U + u, u % UA
                        act.wait_ge(turned_ready, n + 1)
                        act.wait_ge(used, n + 1 + U - UA)
                        act.copy(turned_sb[:, v, :], turned[v % 2][:, 0:P])
                        act.copy(attr_t[:, v, :], turned[v % 2][0:DE, P:2 * P]).then_inc(copied, 1)
                    for u in range(h * UA, (h + 1) * UA):
                        n, v = i * U + u, u % UA
                        act.wait_ge(pre_ready, n + 3)
                        act.activation(hid[:, v, 0:D], pre[:, v, :], ACT.Relu).then_inc(hid_ready, 1)

        @block.gpsimd
        def _(pool):
            with pool.Fori(0, TP // U) as i:
                for h in range(2):
                    pool.wait_ge(staged, i * 2 + h + 1)
                    pool.wait_ge(used, i * U + h * HU + HU)
                    pool.sem_inc(settled, 1)
                    for u in range(h * HU, (h + 1) * HU):
                        pool.indirect_dma_start(
                            out=rows[:, u, :], out_offset=None, in_=p_table,
                            in_offset=bass.IndirectOffsetOnAxis(ap=stage[:, u:u + 1], axis=0)).then_inc(gathered[u], 16)

        @block.tensor
        def _(pe):
            pe.sem_inc(used, U)
            with pe.Fori(0, TP // U) as i:
                for h in range(2):
                    for u in range(h * UA, (h + 1) * UA):
                        n, v = i * U + u, u % UA
                        if v == 0:
                            pe.wait_ge(attr_in[h], i * 16 + 16)
                        pe.wait_ge(hot, n + 1)
                        pe.wait_ge(copied, n + 1)
                        pe.transpose(turned[v % 2][:, 0:P], onehot[:, u, :], k.ident[:, :])
                        pe.transpose(turned[v % 2][0:DE, P:2 * P], attr[:, u, :], k.ident[:, :]).then_inc(turned_ready, 1)
                    for u in range(h * UA, (h + 1) * UA):
                        n, v = i * U + u, u % UA
                        b = pe.value_load(k.tile_block[1][0:1, ds(n, 1)], min_val=0, max_val=NB - 1)
                        pe.wait_ge(copied, n + 3)
                        pe.wait_ge(pre_ready, n + 1)
                        pe.matmul(local[v % 2][:, 0:D], turned_sb[:, v, :],
                                  k.acc2[:, ds(b, 1), :].rearrange("p o d -> p (o d)"), start=True, stop=False)
                        pe.matmul(local[v % 2][:, 0:D], attr_t[:, v, :], k.w_edge[:, :], start=False, stop=True)\
                          .then_inc(local_ready, 1)
                    for u in range(h * UA, (h + 1) * UA):
                        n, v = i * U + u, u % UA
                        pe.wait_ge(hid_ready, n + 1)
                        pe.wait_ge(added, n + 1)
                        pe.matmul(part[v % 2][:, 0:D + 1], onehot[:, u, :], hid[:, v, :], start=True, stop=True)\
                          .then_inc(used, 1)

        @block.vector
        def _(dve):
            dve.memset(k.acc[:, :, :], 0.0).then_inc(zeroed, 1)
            dve.memset(hid[:, :, D:D + 1], 1.0).then_inc(zeroed, 1)
            dve.wait_ge(zeroed, 2)
            for s in (copied, pre_ready, added):
                dve.sem_inc(s, 2)
            with dve.Fori(0, TP // U) as i:
                for h in range(2):
                    for u in range(h * UA, (h + 1) * UA):
                        n = i * U + u
                        dve.wait_ge(used, n + 1)
                        dve.tensor_scalar(onehot[:, u, :], k.lanes[:, :], k.nodes[1][:, ds(n, 1), 0], None,
                                          ALU.is_equal).then_inc(hot, 1)
                    for u in range(h * UA, (h + 1) * UA):
                        n, v = i * U + u, u % UA
                        dve.wait_ge(local_ready, n + 1)
                        dve.wait_ge(gathered[u], i * 16 + 16)
                        dve.tensor_tensor(pre[:, v, :], rows[:, u, :], local[v % 2][:, 0:D], ALU.add)\
                           .then_inc(pre_ready, 1)
                    for u in range(h * UA, (h + 1) * UA):
                        n, v = i * U + u, u % UA
                        b = dve.value_load(k.tile_block[1][0:1, ds(n, 1)], min_val=0, max_val=NB - 1)
                        dve.wait_ge(added, n + 2)
                        dve.wait_ge(used, n + 1 + U)
                        dve.tensor_tensor(k.acc[:, ds(b, 1), 0:D + 1], k.acc[:, ds(b, 1), 0:D + 1],
                                          part[v % 2][:, 0:D + 1].unsqueeze(1), ALU.add).then_inc(added, 1)
    ph.end()


def finish(nc, k, x2_table, agg3, out_table, out):
    ph = Phase(nc)
    norm = Norm(ph)
    x2, ag = ph.sb("x2", [P, 2, NBLK, D], F32), ph.sb("ag", [P, 2, NBLK, D], F32)
    ab = ph.sb("ab", [P, NBLK, D + 1], F32)
    y, z = ph.sb("y", [P, NBLK, D], F32), ph.sb("z", [P, NBLK, D], F32)
    x3, outb = ph.sb("x3", [P, NBLK, D], F32), ph.sb("outb", [P, 2, NBLK, D], F32)
    tA, tB = ph.sb("tA", [P, NBLK, D], F32), ph.sb("tB", [P, NBLK, D], F32)
    cn = ph.sb("cn", [1, NBLK, P], F32)
    free = k.acc2[:, :, :].rearrange("p a b -> p (a b)")
    SZ = 2 * NBLK * P
    act_in, sig = (free[:, n * SZ:(n + 1) * SZ].rearrange("p (a b c) -> p a b c", a=2, b=NBLK) for n in range(2))
    bigA, bigB, bigC = ph.ps("bigA", [P, 2, 512]), ph.ps("bigB", [P, 2, 512]), ph.ps("bigC", [P, 2, 512])
    cnt_ps = ph.ps("cnt_ps", [1, 2, 512])
    loaded, stored = [ph.sem("loaded0"), ph.sem("loaded1")], [ph.sem("stored0"), ph.sem("stored1")]
    chain = ph.sem("chain")
    sums_in, turned, turned_out = ph.sem("sums_in"), ph.sem("turned"), ph.sem("turned_out")
    agg_ready, agg_out, upd_ready = ph.sem("agg_ready"), ph.sem("agg_out"), ph.sem("upd_ready")
    x3_ready, x3_turned, x3_out = ph.sem("x3_ready"), ph.sem("x3_turned"), ph.sem("x3_out")
    up_ready, up_out, hid_ready = ph.sem("up_ready"), ph.sem("up_out"), ph.sem("hid_ready")
    down_ready, out_ready, copied_out = ph.sem("down_ready"), ph.sem("out_ready"), ph.sem("copied_out")
    settled = ph.sem("settled")
    flat = lambda t: t.rearrange("p a b -> p (a b)")
    with nc.Block() as block:
        @block.sync
        def _(sp):
            with sp.Fori(0, NR // 2) as i:
                for r in range(2):
                    b = ds((i * 2 + r) * NBLK, NBLK)
                    sp.wait_ge(stored[r], i * 16)
                    sp.dma_start(x2[:, r], blocks_of(x2_table)[:, b, :]).then_inc(loaded[r], 16)
                    sp.dma_start(ag[:, r], blocks_of(agg3)[:, b, :]).then_inc(loaded[r], 16)
            for r in range(2):
                sp.wait_ge(stored[r], NR // 2 * 16)
            sp.dma_start(out, out_table[0:N, :]).then_inc(copied_out, 16)
            sp.wait_ge(copied_out, 16)

        @block.gpsimd
        def _(pool):
            with pool.Fori(0, NR // 2) as i:
                for r in range(2):
                    pool.wait_ge(out_ready, i * 2 + r + 1)
                    pool.sem_inc(settled, 1)
                    pool.dma_start(blocks_of(out_table)[:, ds((i * 2 + r) * NBLK, NBLK), :], outb[:, r])\
                        .then_inc(stored[r], 16)

        @block.scalar
        def _(act):
            with act.Fori(0, NR // 2) as i:
                for r in range(2):
                    R = i * 2 + r
                    act.wait_ge(turned, R)
                    act.copy(ab[:, :, :], k.acc[:, ds(R * NBLK, NBLK), 0:D + 1]).then_inc(sums_in, 1)
                    act.wait_ge(turned, R + 1)
                    for sl, ps in banks(bigA):
                        act.copy(tA[:, sl, :], ps)
                    for sl, ps in banks(cnt_ps):
                        ins = act.copy(cn[:, sl, :], ps)
                    ins.then_inc(turned_out, 1)
                    act.wait_ge(agg_ready, R + 1)
                    for sl, ps in banks(bigB):
                        ins = act.copy(tB[:, sl, :], ps)
                    ins.then_inc(agg_out, 1)
                    norm.root(act, R * 4 + 1)
                    norm.root(act, R * 4 + 2)
                    act.wait_ge(x3_turned, R + 1)
                    for sl, ps in banks(bigA):
                        act.copy(tA[:, sl, :], ps)
                    for sl, ps in banks(bigB):
                        ins = act.copy(tB[:, sl, :], ps)
                    ins.then_inc(x3_out, 1)
                    for m in range(2):
                        act.wait_ge(up_ready, R * 2 + m + 1)
                        for sl, ps in banks((bigA, bigC)[m]):
                            act.activation(act_in[:, m, sl, :], ps, ACT.Identity, bias=k.b_up[:, m:m + 1])
                        for sl, ps in banks((bigA, bigC)[m]):
                            ins = act.activation(sig[:, m, sl, :], ps, ACT.Sigmoid, bias=k.b_up[:, m:m + 1])
                        ins.then_inc(up_out, 1)
                    norm.root(act, R * 4 + 3)
                    norm.root(act, R * 4 + 4)

        @block.tensor
        def _(pe):
            with pe.Fori(0, NR // 2) as i:
                for r in range(2):
                    R = i * 2 + r
                    pe.wait_ge(sums_in, R + 1)
                    pe.wait_ge(up_out, R * 2)
                    for j in range(NBLK):
                        pe.transpose(bank(bigA, j), ab[:, j, 0:D], k.ident[:, :])
                        ins = pe.matmul(bank(cnt_ps, j), ab[:, j, D:D + 1], k.ident[:, :], start=True, stop=True)
                    ins.then_inc(turned, 1)
                    pe.wait_ge(turned_out, R + 1)
                    pe.wait_ge(down_ready, R)
                    for j in range(NBLK):
                        pe.matmul(bank(bigB, j), k.w_out[:, :], tA[:, j, :], start=True, stop=False)
                        ins = pe.matmul(bank(bigB, j), k.b_out[:, :], cn[:, j, :], start=False, stop=True)
                    ins.then_inc(agg_ready, 1)
                    pe.wait_ge(agg_out, R + 1)
                    pe.wait_ge(out_ready, R)
                    for j in range(NBLK):
                        pe.matmul(bank(bigC, j), tB[:, j, :], k.w_upd[:, :], start=True, stop=False)
                        ins = pe.matmul(bank(bigC, j), k.ones[0:1, :], k.b_upd[:, :], start=False, stop=True)
                    ins.then_inc(upd_ready, 1)
                    pe.wait_ge(loaded[r], i * 32 + 32)
                    for j in range(NBLK):
                        pe.transpose(bank(bigB, j), ag[:, r, j, :], k.ident[:, :])
                    pe.wait_ge(x3_ready, R + 1)
                    for j in range(NBLK):
                        ins = pe.transpose(bank(bigA, j), x3[:, j, :], k.ident[:, :])
                    ins.then_inc(x3_turned, 1)
                    pe.wait_ge(x3_out, R + 1)
                    for m in range(2):
                        ps = (bigA, bigC)[m]
                        for j in range(NBLK):
                            pe.matmul(bank(ps, j), k.w_up[:, 0, m * P:(m + 1) * P], tA[:, j, :], start=True, stop=False)
                            ins = pe.matmul(bank(ps, j), k.w_up[:, 1, m * P:(m + 1) * P], tB[:, j, :],
                                            start=False, stop=True)
                        ins.then_inc(up_ready, 1)
                    pe.wait_ge(hid_ready, R + 1)
                    for j in range(NBLK):
                        for m in range(2):
                            pe.matmul(bank(bigB, j), act_in[:, m, j, :], k.w_down[:, m, :], start=(m == 0), stop=False)
                        ins = pe.matmul(bank(bigB, j), k.ones[0:1, :], k.b_down[:, :], start=False, stop=True)
                    ins.then_inc(down_ready, 1)

        @block.vector
        def _(dve):
            link = Chain(dve, chain)

            def affine(t, n):
                link(dve.tensor_tensor(t, t, k.scales[:, 2 * n:2 * n + 1, :].to_broadcast([P, NBLK, D]), ALU.mult))
                link(dve.tensor_tensor(t, t, k.scales[:, 2 * n + 1:2 * n + 2, :].to_broadcast([P, NBLK, D]), ALU.add))

            with dve.Fori(0, NR // 2) as i:
                for r in range(2):
                    R = i * 2 + r
                    link.round(R, 4 * 4 + 2 * 2 + 4)
                    dve.wait_ge(loaded[r], i * 32 + 32)
                    dve.wait_ge(upd_ready, R + 1)
                    for sl, ps in banks(bigC):
                        ins = dve.scalar_tensor_tensor(y[:, sl, :], ps, 0.0, x2[:, r, sl, :], ALU.max, ALU.add)
                    link(ins)
                    norm(dve, link, y, z, R * 4 + 1)
                    affine(z[:, :, :], 0)
                    link(dve.tensor_tensor(z[:, :, :], z[:, :, :], x2[:, r], ALU.add))
                    norm(dve, link, z, x3, R * 4 + 2)
                    dve.nop().then_inc(x3_ready, 1)
                    dve.wait_ge(up_out, R * 2 + 2)
                    dve.tensor_tensor(act_in[:, :, :, :].rearrange("p a b c -> p (a b c)"),
                                      act_in[:, :, :, :].rearrange("p a b c -> p (a b c)"),
                                      sig[:, :, :, :].rearrange("p a b c -> p (a b c)"), ALU.mult).then_inc(hid_ready, 1)
                    dve.wait_ge(down_ready, R + 1)
                    for sl, ps in banks(bigB):
                        ins = dve.tensor_copy(y[:, sl, :], ps)
                    link(ins)
                    norm(dve, link, y, z, R * 4 + 3)
                    affine(z[:, :, :], 1)
                    link(dve.scalar_tensor_tensor(y[:, :, :], x3[:, :, :], 2.0, z[:, :, :], ALU.mult, ALU.add))
                    dve.wait_ge(stored[r], i * 16)
                    norm(dve, link, y, outb[:, r], R * 4 + 4)
                    dve.nop().then_inc(out_ready, 1)
    ph.end()


def layers(nc, k, a, out, upto, sb, dram):
    k.dis = sb("dis", [P, NB], F32)
    k.nodes = [sb("nodes_src", [P, TP, 2], F32), sb("nodes_dst", [P, TP, 2], F32)]
    k.acc = sb("acc", [P, NB, AW], F32)
    k.acc2 = sb("acc2", [P, NB, D], F32)
    k.a1, k.top = sb("a1", [P, NB, H], F32), sb("top", [P, NB, H], F32)
    load_weights(nc, k, a, sb)
    tables = [dram(f"scaled{n}", [NP, D]) for n in range(3)]
    agg3, rest, x2 = dram("agg3", [NP, D]), dram("rest", [NP, D]), dram("x2", [NP, D])
    att, p_table, out_table = dram("att", [NP, AW]), dram("p_table", [NP, D]), dram("out_table", [NP, D])
    fetch_nodes(nc, k)
    scale_nodes(nc, k, k.x_pad, tables[0])
    hop(nc, k, tables[0], k.by_src, agg3, tables[1])
    hop(nc, k, tables[1], None, None, tables[2])
    hop(nc, k, tables[2], None, None, None)
    if upto >= 3:
        to_attention(nc, k, tables[2], k.x_pad, att, rest)
    if upto >= 4:
        attention(nc, k, att)
        to_messages(nc, k, rest, x2, p_table)
    if upto >= 5:
        messages(nc, k, p_table)
        finish(nc, k, x2, agg3, out_table, out)


class Store:
    pass


def build(nc, a, out, upto=99):
    k = Store()
    with ExitStack() as ctx:
        def sb(name, shape, dt):
            return ctx.enter_context(nc.sbuf_tensor(name, shape, dt))

        def dram(name, shape, dt=F32):
            return nc.dram_tensor(name, shape, dt, kind="Internal").ap()

        k.ident = sb("ident", [P, P], F32)
        k.ones = sb("ones", [P, P], F32)
        k.tri = sb("tri", [P, P], F32)
        k.lanes_i = sb("lanes_i", [P, P], I32)
        k.lanes = sb("lanes", [P, P], F32)
        k.lanes_b = sb("lanes_b", [P, P], BF16)
        k.zero_b = sb("zero_b", [P, P], BF16)
        k.tile_block = [sb("tile_block_src", [1, TP], I32), sb("tile_block_dst", [1, TP], I32)]
        k.dis2 = sb("dis2", [P, NB], F32)
        k.by_src = dram("by_src", [TP * P, D + 2])
        k.by_dst = dram("by_dst", [TP * P, DE + 2])
        k.x_pad = dram("x_pad", [NP, D])
        with ExitStack() as early:
            k.tiles_i = early.enter_context(nc.sbuf_tensor("tiles_i", [P, TP], I32))
            k.tiles = early.enter_context(nc.sbuf_tensor("tiles", [P, TP], F32))
            constants(nc, k)
            group_edges(nc, k, a["src"], a["dst"], a["edge_attr_128"], a["edge_attr_32"], a["x"])
        if upto >= 2:
            layers(nc, k, a, out, upto, sb, dram)


_INS = ['x', 'src', 'dst', 'edge_attr_128', 'edge_attr_32', 'L1_gnn_W_l', 'L1_gnn_W_r', 'L1_gnn_a1w', 'L1_gnn_a2w',
        'L1_gnn_bias', 'L2_gnn_W1', 'L2_gnn_b1', 'L2_gnn_W2', 'L2_gnn_b2', 'L2_gnn_Wu', 'L2_gnn_bu', 'L2_gnn_gamma',
        'L2_gnn_beta', 'L3_gnn_W1', 'L3_gnn_b1', 'L3_gnn_W2', 'L3_gnn_b2', 'L3_gnn_ln_gamma', 'L3_gnn_ln_beta']


def kernel(**inputs):
    import numpy as _np
    import concourse.bacc as _bacc
    from concourse import mybir as _mybir
    from concourse.bass_utils import run_bass_kernel_spmd as _run

    nc = _bacc.Bacc("TRN2", target_bir_lowering=False, num_devices=1)
    arrays, args = {}, {}
    for name in _INS:
        a = _np.ascontiguousarray(inputs[name])
        arrays[f"in_{name}_dram"] = a
        args[name] = nc.dram_tensor(f"in_{name}_dram", a.shape, _mybir.dt.from_np(a.dtype), kind="ExternalInput").ap()
    out = nc.dram_tensor("out_0_dram", (N, D), F32, kind="ExternalOutput").ap()
    build(nc, args, out)
    r = _run(nc, [arrays], core_ids=[0])
    return r.results[0]["out_0_dram"]
```

```python
from contextlib import ExitStack

import concourse.bass as bass
from concourse import mybir

ALU = mybir.AluOpType
ACT = mybir.ActivationFunctionType
AX = mybir.AxisListType.X
F32 = mybir.dt.float32
I32 = mybir.dt.int32
I16 = mybir.dt.int16
BF16 = mybir.dt.bfloat16
DVE = mybir.EngineType.DVE
ds = bass.ds

P = 128
N, E, D, DE = 12500, 212500, 128, 32
H, HD = 4, 32
NB = -(-N // P)
NP = NB * P
LASTN = N - (NB - 1) * P
FC = E // P
REST = E - FC * P
COLS = FC + 1
ROW_BITS = 7
TP = 1760
B = 4
RING = 4
SB = 10
G = 5
BU = 14
HALF = FC // SB // 2 * SB
PARTS = ([slice(0, HALF), slice(HALF, COLS)], [slice(0, COLS)])
NBLK = 7
NR = NB // NBLK
AW = D + H
EPS = 1e-5
FAR = 1.0e30
assert FC % SB == 0 and TP % (RING * B) == 0 and TP >= E // P + NB and NB % NBLK == 0


class Phase:

    def __init__(self, nc):
        self.nc = nc
        self.sems = []
        self.stack = ExitStack()

    def sem(self, name):
        s = self.nc.alloc_semaphore(f"{name}_{self.nc.next_id()}")
        self.sems.append(s)
        return s

    def sb(self, name, shape, dt):
        return self.stack.enter_context(self.nc.sbuf_tensor(f"{name}_{self.nc.next_id()}", shape, dt))

    def ps(self, name, shape, dt=F32):
        return self.stack.enter_context(self.nc.psum_tensor(f"{name}_{self.nc.next_id()}", shape, dt))

    def end(self):
        self.nc.clear_and_free_semaphores(self.sems)
        self.nc.all_engine_barrier()
        self.stack.close()


class Chain:

    def __init__(self, eng, sem):
        self.eng, self.sem, self.n, self.base = eng, sem, 0, 0

    def __call__(self, ins):
        ins.then_inc(self.sem, 1)
        self.n += 1
        self.eng.wait_ge(self.sem, self.base + self.n)

    def round(self, i, steps):
        self.base, self.n = i * steps, 0


def rounds(eng, n):
    yield 0
    with eng.Fori(1, n) as i:
        yield i


def later(i):
    return not isinstance(i, int)


def bc(ap, axis, n):
    return ap.unsqueeze(axis).to_broadcast([*ap.shape[:axis], n, *ap.shape[axis:]])


def constants(nc, k):
    ph = Phase(nc)
    made = ph.sem("made")
    block = nc.Block()
    with block as block:
        @block.gpsimd
        def _(pool):
            pool.memset(k.ident[:, :], 0.0).then_inc(made, 1)
            pool.memset(k.ones[:, :], 1.0).then_inc(made, 1)
            pool.memset(k.tri[:, :], 1.0).then_inc(made, 1)
            pool.memset(k.zero_b[:, :], 0.0).then_inc(made, 1)
            pool.iota(k.lanes_i[:, :], [[1, P]], base=0, channel_multiplier=0).then_inc(made, 1)
            pool.iota(k.tiles_i[:, :], [[1, TP]], base=0, channel_multiplier=0).then_inc(made, 1)
            pool.wait_ge(made, 6)
            pool.affine_select(out=k.ident[:, :], in_=k.ident[:, :], compare_op=ALU.not_equal, fill=1.0,
                               base=0, pattern=[[-1, P]], channel_multiplier=1).then_inc(made, 1)
            pool.affine_select(out=k.tri[:, :], in_=k.tri[:, :], compare_op=ALU.is_gt, fill=0.0,
                               base=0, pattern=[[1, P]], channel_multiplier=-1).then_inc(made, 1)
            pool.wait_ge(made, 8)

        @block.vector
        def _(dve):
            dve.wait_ge(made, 8)
            dve.tensor_copy(k.lanes[:, :], k.lanes_i[:, :])
            dve.tensor_copy(k.lanes_b[:, :], k.lanes_i[:, :])
            dve.tensor_copy(k.tiles[:, :], k.tiles_i[:, :])
    ph.end()


def group_edges(nc, k, src, dst, ea128, ea32, x):
    ph = Phase(nc)
    sb = ph.sb
    raw = [sb("raw_src", [P, COLS], I32), sb("raw_dst", [P, COLS], I32)]
    lo = [sb("lo_src", [P, COLS], F32), sb("lo_dst", [P, COLS], F32)]
    hi = [sb("hi_src", [P, COLS], F32), sb("hi_dst", [P, COLS], F32)]
    hi_b = [sb("hi_b_src", [P, COLS], BF16), sb("hi_b_dst", [P, COLS], BF16)]
    slot = [sb("slot_src", [P, COLS], I32), sb("slot_dst", [P, COLS], I32)]
    ti = sb("ti", [P, COLS], I32)
    hit = [sb("hit0", [P, COLS], BF16), sb("hit1", [P, COLS], BF16)]
    run = [sb("run0", [P, COLS], F32), sb("run1", [P, COLS], F32)]
    pos = sb("pos", [P, COLS], F32)
    hist = sb("hist", [P, NB], F32)
    cnt = sb("cnt", [P, NB], F32)
    cnt_i = sb("cnt_i", [P, NB], I32)
    tls = sb("tls", [P, NB], F32)
    tend = sb("tend", [P, NB], F32)
    base = sb("base", [P, NB], F32)
    ecol = sb("ecol", [P, 1], F32)
    past = sb("past", [P, TP], F32)
    tb_f = sb("tb_f", [1, TP], F32)
    W = [D + 2, DE + 2]
    table = [k.by_src, k.by_dst]
    data = [ea128, ea32]
    pay = [sb("pay_src", [P, SB, W[0]], F32), sb("pay_dst", [P, SB, W[1]], F32)]
    stage = [sb("stage_src", [P, SB], I32), sb("stage_dst", [P, SB], I32)]
    FR = 40
    fill = [sb("fill_src", [P, FR, W[0]], F32), None]
    fill[1] = fill[0][:, :, :].rearrange("p a b -> p (a b)")[:, 0:FR * W[1]].rearrange("p (a b) -> p a b", a=FR)
    fill[0] = fill[0][:, :, :]
    ohl = sb("ohl", [P, 2, G, P], BF16)
    ohh = sb("ohh", [P, 2, G, NB], BF16)
    zb = sb("zb", [P, P], BF16)
    tot_ps, pre_ps, tb_ps = ph.ps("tot", [P, NB]), ph.ps("pre", [P, NB]), ph.ps("tb", [1, 4, 512])
    deg_ps = ph.ps("deg", [P, NB])

    keys_in, fill_set, filled = ph.sem("keys_in"), ph.sem("fill_set"), ph.sem("filled")
    filled2, raw_set, fill2_set = ph.sem("filled2"), ph.sem("raw_set"), ph.sem("fill2_set")
    x_out, nodes_in = ph.sem("x_out"), ph.sem("nodes_in")
    chain, hist_ready, sums_ready = ph.sem("chain"), ph.sem("hist_ready"), ph.sem("sums_ready")
    past_ready, tb_ready, slots_ready = ph.sem("past_ready"), ph.sem("tb_ready"), ph.sem("slots_ready")
    pay_in = [[ph.sem(f"pay_in{s}{g}") for g in range(2)] for s in range(2)]
    cols_set = [[ph.sem(f"cols_set{s}{g}") for g in range(2)] for s in range(2)]
    scattered = [[ph.sem(f"scattered{s}{g}") for g in range(2)] for s in range(2)]
    settled, settled_dve = ph.sem("settled"), ph.sem("settled_dve")
    oh_ready, oh_used, deg_ready = ph.sem("oh_ready"), ph.sem("oh_used"), ph.sem("deg_ready")

    with nc.Block() as block:
        @block.sync
        def _(sp):
            sp.wait_ge(raw_set, 2)
            for s, key in enumerate((src, dst)):
                sp.dma_start(raw[s][:, 0:FC], key[0:FC * P].rearrange("(p c) -> p c", p=P)).then_inc(keys_in, 16)
                sp.dma_start(raw[s][0:REST, FC:COLS],
                             key[FC * P:E].rearrange("(p c) -> p c", c=1)).then_inc(keys_in, 16)
            sp.wait_ge(fill_set, 2)
            sp.dma_start(k.x_pad[0:N, :], x).then_inc(x_out, 16)
            sp.dma_start(k.x_pad[N:NP, :], fill[0][0:NP - N, 0, 0:D]).then_inc(x_out, 16)
            sp.wait_ge(x_out, 32)
            for s in range(2):
                rows = data[s][0:FC * P, :].rearrange("(p c) w -> p c w", p=P)
                w = W[s] - 2
                for i in rounds(sp, FC // SB):
                    for g in range(2):
                        if later(i):
                            sp.wait_ge(scattered[s][g], i * (16 * G))
                        sp.dma_start(pay[s][:, g * G:(g + 1) * G, 0:w],
                                     rows[:, ds(i * SB + g * G, G), :]).then_inc(pay_in[s][g], 16)
                sp.wait_ge(scattered[s][0], FC // 2 * 16)
                sp.dma_start(pay[s][0:REST, 0, 0:w], data[s][FC * P:E, :]).then_inc(pay_in[s][0], 16)

        @block.scalar
        def _(act):
            def put_columns(s, i):
                for g in range(2):
                    c = ds(i * SB + g * G, G)
                    b = slice(g * G, (g + 1) * G)
                    if later(i):
                        act.wait_ge(scattered[s][g], i * (16 * G))
                    act.copy(stage[s][:, b], slot[s][:, c])
                    act.copy(pay[s][:, b, W[s] - 2], lo[s][:, c])
                    act.copy(pay[s][:, b, W[s] - 1].bitcast(I32), raw[1 - s][:, c]).then_inc(cols_set[s][g], 1)

            act.wait_ge(fill_set, 2)
            for c in range(TP // FR):
                act.dma_start(table[0].rearrange("(p r) w -> p r w", p=P)[:, c * FR:(c + 1) * FR, :],
                              fill[0]).then_inc(filled, 16)
            act.wait_ge(filled, 16 * (TP // FR))
            act.nop().then_inc(fill2_set, 1)
            act.wait_ge(fill2_set, 3)
            for c in range(TP // FR):
                act.dma_start(table[1].rearrange("(p r) w -> p r w", p=P)[:, c * FR:(c + 1) * FR, :],
                              fill[1]).then_inc(filled2, 16)
            for s in range(2):
                act.wait_ge(slots_ready, sum(len(p) for p in PARTS[:s]) + 1)
                for i in rounds(act, PARTS[s][0].stop // SB):
                    put_columns(s, i)
                if len(PARTS[s]) > 1:
                    act.wait_ge(slots_ready, len(PARTS[0]))
                    with act.Fori(PARTS[s][0].stop // SB, FC // SB) as i:
                        put_columns(s, i)
                act.wait_ge(scattered[s][0], FC // 2 * 16)
                act.copy(stage[s][:, 0:1], slot[s][:, FC:COLS])
                act.copy(pay[s][:, 0, W[s] - 2:W[s] - 1], lo[s][:, FC:COLS])
                act.copy(pay[s][:, 0, W[s] - 1:W[s]].bitcast(I32), raw[1 - s][:, FC:COLS]).then_inc(cols_set[s][0], 1)
                if s == 0:
                    act.wait_ge(scattered[s][0], FC // 2 * 16 + 16)
                    act.wait_ge(scattered[s][1], FC // 2 * 16)
                    act.dma_start(k.nodes[0][:, 0:TP, :], table[0].rearrange("(t p) w -> p t w", p=P)[:, :, D:D + 2])\
                       .then_inc(nodes_in, 16)
            act.wait_ge(nodes_in, 16)

        @block.gpsimd
        def _(pool):
            pool.memset(raw[0][:, FC:COLS], -1).then_inc(raw_set, 1)
            pool.memset(raw[1][:, FC:COLS], -1).then_inc(raw_set, 1)
            pool.memset(fill[0], 0.0).then_inc(chain_pool := ph.sem("chain_pool"), 1)
            pool.wait_ge(chain_pool, 1)
            pool.memset(fill[0][:, :, W[0] - 2:W[0] - 1], -1.0).then_inc(fill_set, 2)
            pool.wait_ge(fill2_set, 1)
            pool.wait_ge(x_out, 32)
            pool.memset(fill[1], 0.0).then_inc(fill2_set, 1)
            pool.wait_ge(fill2_set, 2)
            pool.memset(fill[1][:, :, W[1] - 2:W[1] - 1], -1.0).then_inc(fill2_set, 1)

            def put(s, j, rows=P):
                pool.indirect_dma_start(
                    out=table[s], out_offset=bass.IndirectOffsetOnAxis(ap=stage[s][0:rows, j:j + 1], axis=0),
                    in_=pay[s][0:rows, j, :], in_offset=None).then_inc(scattered[s][j // G], 16)

            for s in range(2):
                with pool.Fori(0, FC // SB) as i:
                    for g in range(2):
                        pool.wait_ge(cols_set[s][g], i + 1)
                        pool.wait_ge(pay_in[s][g], i * 16 + 16)
                        pool.wait_ge([filled, filled2][s], 16 * (TP // FR))
                        pool.sem_inc(settled, 1)
                        for j in range(g * G, (g + 1) * G):
                            put(s, j)
                pool.wait_ge(cols_set[s][0], FC // SB + 1)
                pool.wait_ge(pay_in[s][0], FC // SB * 16 + 16)
                put(s, 0, REST)
                pool.wait_ge(scattered[s][0], FC // 2 * 16 + 16)
                pool.wait_ge(scattered[s][1], FC // 2 * 16)

        @block.vector
        def _(dve):
            link = Chain(dve, chain)

            def rank(s, c):
                n = c.stop - c.start

                def mark(j, b):
                    return dve.tensor_scalar(hit[j % 2][:, 0:n], hi_b[s][:, c], k.lanes[:, ds(b, 1)], None, ALU.is_equal)

                done = link.n + 1
                link(mark(0, 0))
                with dve.Fori(0, NB // BU) as i:
                    for j in range(BU):
                        b = i * BU + j
                        dve.wait_ge(chain, done + b * 4 - 2)
                        dve.tensor_tensor_scan(run[j % 2][:, 0:n], hit[j % 2][:, 0:n], hit[j % 2][:, 0:n],
                                               base[:, ds(b, 1)], ALU.add, ALU.max).then_inc(chain, 1)
                        dve.wait_ge(chain, done + b * 4)
                        mark(j + 1, b + 1).then_inc(chain, 1)
                        dve.wait_ge(chain, done + b * 4 + 1)
                        dve.sem_inc(settled_dve, 1)
                        dve.copy_predicated(pos[:, c], hit[j % 2][:, 0:n].bitcast(I16), run[j % 2][:, 0:n])\
                           .then_inc(chain, 1)
                        dve.tensor_scalar(base[:, ds(b, 1)], run[j % 2][:, n - 1:n], 0.0, None, ALU.add)\
                           .then_inc(chain, 1)
                link.n = done + NB * 4
                dve.wait_ge(chain, link.n)

            dve.wait_ge(keys_in, 64)
            for s in range(2):
                link(dve.tensor_scalar(ti[:, :], raw[s][:, :], ROW_BITS, None, ALU.arith_shift_right))
                dve.tensor_copy(hi[s][:, :], ti[:, :])
                link(dve.tensor_copy(hi_b[s][:, :], ti[:, :]))
                link(dve.tensor_scalar(ti[:, :], raw[s][:, :], P - 1, None, ALU.bitwise_and))
                link(dve.tensor_copy(lo[s][:, :], ti[:, :]))
            for s in range(2):
                done = link.n
                with dve.Fori(0, NB // BU) as i:
                    for j in range(BU):
                        b = i * BU + j
                        dve.wait_ge(chain, done + b - 1)
                        dve.tensor_scalar(hit[j % 2][:, :], hi_b[s][:, :], k.lanes[:, ds(b, 1)], 0.0,
                                          ALU.is_equal, ALU.add, accum_out=hist[:, ds(b, 1)]).then_inc(chain, 1)
                link.n = done + NB
                dve.wait_ge(chain, link.n)
                dve.nop().then_inc(hist_ready, 1)
                dve.wait_ge(sums_ready, s + 1)
                link(dve.tensor_scalar(cnt_i[:, :], tot_ps[:, :], float(P - 1), None, ALU.add))
                link(dve.tensor_scalar(cnt_i[:, :], cnt_i[:, :], ROW_BITS, None, ALU.arith_shift_right))
                link(dve.tensor_copy(tls[:, :], cnt_i[:, :]))
                link(dve.memset(cnt[:, :], 0.0))
                link(dve.tensor_tensor_scan(tend[:, :], tls[:, :], cnt[:, :], 0.0, ALU.add, ALU.max))
                link(dve.tensor_tensor(tls[:, :], tend[:, :], tls[:, :], ALU.subtract))
                link(dve.scalar_tensor_tensor(base[:, :], tls[:, :], float(P), pre_ps[:, :], ALU.mult, ALU.add))
                link(dve.tensor_tensor(cnt[:, :], tend[:, :], k.ident[:, 0:NB], ALU.mult))
                link(dve.tensor_reduce(ecol[:, :], cnt[:, :], AX, ALU.add))
                dve.tensor_scalar(past[:, :], k.tiles[:, :], ecol[:, 0:1], None, ALU.is_ge).then_inc(past_ready, 1)
                dve.wait_ge(tb_ready, s + 1)
                link(dve.tensor_scalar(tb_f[:, :].rearrange("a (b c) -> a b c", b=4), tb_ps[:, :, 0:TP // 4],
                                       float(NB - 1), None, ALU.min))
                link(dve.tensor_copy(k.tile_block[s][:, :], tb_f[:, :]))
                link(dve.memset(pos[:, :], 0.0))
                for c in PARTS[s]:
                    rank(s, c)
                    dve.tensor_scalar(slot[s][:, c], pos[:, c], -1.0, None, ALU.add).then_inc(slots_ready, 1)
                dve.wait_ge(slots_ready, sum(len(p) for p in PARTS[:s + 1]))
            with dve.Fori(0, FC // SB) as i:
                for g in range(2):
                    dve.wait_ge(oh_used, i * 2 + g + 1)
                    for j in range(G):
                        c = i * SB + g * G + j
                        dve.tensor_scalar(ohl[:, g, j, :], k.lanes_b[:, :], lo[0][:, ds(c, 1)], None, ALU.is_equal)
                        ins = dve.tensor_scalar(ohh[:, g, j, :], k.lanes_b[:, 0:NB], hi[0][:, ds(c, 1)], None,
                                                ALU.is_equal)
                    ins.then_inc(oh_ready, 1)
            dve.wait_ge(oh_used, FC // G + 1)
            dve.tensor_scalar(ohl[:, 0, 0, :], k.lanes_b[:, :], lo[0][:, FC:COLS], None, ALU.is_equal)
            dve.tensor_scalar(ohh[:, 0, 0, :], k.lanes_b[:, 0:NB], hi[0][:, FC:COLS], None,
                              ALU.is_equal).then_inc(oh_ready, 1)
            dve.wait_ge(deg_ready, 1)
            link(dve.tensor_scalar(cnt[:, :], deg_ps[:, :], 1.0, 1.0, ALU.add, ALU.max))
            link(dve.reciprocal(k.dis2[:, :], cnt[:, :]))

        @block.tensor
        def _(pe):
            for s in range(2):
                pe.wait_ge(hist_ready, s + 1)
                pe.matmul(tot_ps[:, :], k.ones[:, :], hist[:, :], start=True, stop=True)
                pe.matmul(pre_ps[:, :], k.tri[:, :], hist[:, :], start=True, stop=True).then_inc(sums_ready, 1)
                pe.wait_ge(past_ready, s + 1)
                for c in range(4):
                    ins = pe.matmul(tb_ps[:, c, 0:TP // 4], k.ones[0:NB, 0:1],
                                    past[0:NB, c * (TP // 4):(c + 1) * (TP // 4)], start=True, stop=True)
                ins.then_inc(tb_ready, 1)
            pe.wait_ge(fill_set, 2)
            pe.matmul(deg_ps[:, :], k.zero_b[:, :], k.lanes_b[:, 0:NB], start=True, stop=False,
                      skip_group_check=True)
            pe.sem_inc(oh_used, 2)
            with pe.Fori(0, FC // SB) as i:
                for g in range(2):
                    pe.wait_ge(oh_ready, i * 2 + g + 1)
                    for j in range(G):
                        ins = pe.matmul(deg_ps[:, :], ohl[:, g, j, :], ohh[:, g, j, :], start=False, stop=False,
                                        skip_group_check=True)
                    ins.then_inc(oh_used, 1)
            pe.wait_ge(oh_ready, FC // G + 1)
            pe.matmul(deg_ps[:, :], ohl[:, 0, 0, :], ohh[:, 0, 0, :], start=False, stop=True,
                      skip_group_check=True).then_inc(deg_ready, 1)
    ph.end()


def load_weights(nc, k, a, sb):
    k.w_att = sb("w_att", [P, 2 * D + 2 * H], F32)
    k.b_att = sb("b_att", [P, D], F32)
    k.w_msg = sb("w_msg", [P, 2 * D], F32)
    k.b_msg = sb("b_msg", [P, D], F32)
    k.w_edge = sb("w_edge", [DE, D], F32)
    k.w_out = sb("w_out", [P, D], F32)
    k.b_out = sb("b_out", [1, D], F32)
    k.w_upd = sb("w_upd", [P, D], F32)
    k.b_upd = sb("b_upd", [1, D], F32)
    k.w_up = sb("w_up", [P, 2, 2 * D], F32)
    k.b_up = sb("b_up", [P, 2], F32)
    k.w_down = sb("w_down", [P, 2, D], F32)
    k.b_down = sb("b_down", [1, D], F32)
    k.scales = sb("scales", [P, 4, D], F32)
    ph = Phase(nc)
    w1, w2, wu = ph.sb("w1", [P, 2 * D + DE], F32), ph.sb("w2", [P, D], F32), ph.sb("wu", [P, D], F32)
    turned = ph.ps("turned", [P, 5, 512])
    loaded, turned_ready = ph.sem("loaded"), ph.sem("turned_ready")
    row = lambda v: v.rearrange("(a d) -> a d", a=1)
    c0, c1, c2 = D, D + H, D + 2 * H
    parts = [
        (k.w_att[:, 0:c0], a["L1_gnn_W_l"]), (k.w_att[:, c0:c1], a["L1_gnn_a2w"]),
        (k.w_att[:, c1:c2], a["L1_gnn_a1w"]), (k.w_att[:, c2:], a["L1_gnn_W_r"]),
        (k.b_att[:, :], row(a["L1_gnn_bias"]).to_broadcast([P, D])),
        (k.b_msg[:, :], row(a["L2_gnn_b1"]).to_broadcast([P, D])),
        (k.b_out[:, :], row(a["L2_gnn_b2"])), (k.b_upd[:, :], row(a["L2_gnn_bu"])),
        (k.w_up[:, :, :], a["L3_gnn_W1"].rearrange("(h p) m -> p h m", p=P)),
        (k.w_down[:, :, :], a["L3_gnn_W2"].rearrange("(h p) m -> p h m", p=P)),
        (k.b_down[:, :], row(a["L3_gnn_b2"])),
        (w1[:, :], a["L2_gnn_W1"]), (w2[:, :], a["L2_gnn_W2"]), (wu[:, :], a["L2_gnn_Wu"]),
        *[(k.b_up[:, h:h + 1], a["L3_gnn_b1"][h * P:(h + 1) * P].rearrange("(p o) -> p o", o=1)) for h in range(2)],
        *[(k.scales[:, n, :], row(a[v]).to_broadcast([P, D])) for n, v in enumerate(
            ("L2_gnn_gamma", "L2_gnn_beta", "L3_gnn_ln_gamma", "L3_gnn_ln_beta"))],
    ]
    with nc.Block() as block:
        @block.sync
        def _(sp):
            for to, of in parts:
                sp.dma_start(to, of).then_inc(loaded, 16)
            sp.wait_ge(loaded, 16 * len(parts))

        @block.tensor
        def _(pe):
            pe.wait_ge(loaded, 16 * len(parts))
            pe.transpose(turned[:, 0, 0:P], w1[:, 0:D], k.ident[:, :])
            pe.transpose(turned[:, 1, 0:P], w1[:, D:2 * D], k.ident[:, :])
            pe.transpose(turned[0:DE, 2, 0:P], w1[:, 2 * D:], k.ident[:, :])
            pe.transpose(turned[:, 3, 0:P], w2[:, :], k.ident[:, :])
            pe.transpose(turned[:, 4, 0:P], wu[:, :], k.ident[:, :]).then_inc(turned_ready, 1)

        @block.vector
        def _(dve):
            dve.wait_ge(turned_ready, 1)
            for to, n in ((k.w_msg[:, 0:D], 0), (k.w_msg[:, D:], 1), (k.w_edge[:, :], 2), (k.w_out[:, :], 3),
                          (k.w_upd[:, :], 4)):
                dve.tensor_copy(to, turned[0:to.shape[0], n, 0:P])
    ph.end()


def blocks_of(table):
    return table.rearrange("(b p) d -> p b d", p=P)


def scale_nodes(nc, k, x, scaled):
    ph = Phase(nc)
    xb, gb = ph.sb("xb", [P, 2, NBLK, D], F32), ph.sb("gb", [P, 2, NBLK, D], F32)
    root, dis_ready = ph.sem("root"), ph.sem("dis_ready")
    loaded, stored = [ph.sem("loaded0"), ph.sem("loaded1")], [ph.sem("stored0"), ph.sem("stored1")]
    made = ph.sem("made")
    with nc.Block() as block:
        @block.sync
        def _(sp):
            for i in rounds(sp, NR // 2):
                for r in range(2):
                    if later(i):
                        sp.wait_ge(stored[r], i * 16)
                    sp.dma_start(xb[:, r], blocks_of(x)[:, ds((i * 2 + r) * NBLK, NBLK), :]).then_inc(loaded[r], 16)

        @block.scalar
        def _(act):
            act.activation(k.dis[:, :], k.dis2[:, :], ACT.Sqrt).then_inc(dis_ready, 1)
            for i in rounds(act, NR // 2):
                for r in range(2):
                    act.wait_ge(made, i * 2 + r + 1)
                    act.dma_start(blocks_of(scaled)[:, ds((i * 2 + r) * NBLK, NBLK), :], gb[:, r]).then_inc(stored[r], 16)
            for r in range(2):
                act.wait_ge(stored[r], NR // 2 * 16)

        @block.vector
        def _(dve):
            for s in range(2):
                dve.memset(k.nodes[s][:, TP:, :], 0.0)
            dve.wait_ge(dis_ready, 1)
            for i in rounds(dve, NR // 2):
                for r in range(2):
                    dve.wait_ge(loaded[r], i * 16 + 16)
                    if later(i):
                        dve.wait_ge(stored[r], i * 16)
                    for j in range(NBLK):
                        ins = dve.tensor_scalar(gb[:, r, j], xb[:, r, j], k.dis[:, ds((i * 2 + r) * NBLK + j, 1)],
                                                None, ALU.mult)
                    ins.then_inc(made, 1)
    ph.end()


class Norm:

    def __init__(self, ph):
        self.stats = ph.sb("stats", [P, NBLK, 6], F32)
        self.mv = ph.sb("mv", [P, NBLK, 2], F32)
        self.std = ph.sb("std", [P, NBLK], F32)
        self.rstd = ph.sb("rstd", [P, NBLK], F32)
        self.settled = ph.sem("settled_stats")
        self.var_ready, self.std_ready = ph.sem("var_ready"), ph.sem("std_ready")

    def root(self, act, nth):
        act.wait_ge(self.var_ready, nth)
        act.activation(self.std[:, :], self.rstd[:, :], ACT.Sqrt).then_inc(self.std_ready, 1)

    def __call__(self, dve, link, y, out, nth):
        for j in range(NBLK):
            ins = dve.bn_stats(self.stats[:, j, :], y[:, j, :])
        link(ins)
        dve.sem_inc(self.settled, 1)
        for j in range(NBLK):
            ins = dve.bn_aggr(self.mv[:, j, :], self.stats[:, j, :])
        link(ins)
        dve.tensor_scalar(self.rstd[:, :], self.mv[:, :, 1], EPS, None, ALU.add).then_inc(self.var_ready, 1)
        dve.wait_ge(self.std_ready, nth)
        link(dve.reciprocal(self.rstd[:, :], self.std[:, :]))
        for j in range(NBLK):
            ins = dve.tensor_scalar(out[:, j, :], y[:, j, :], self.mv[:, j, 0:1], self.rstd[:, j:j + 1],
                                    ALU.subtract, ALU.mult)
        link(ins)


def bank(ps, j, n=P):
    return ps[:, j // 4, (j % 4) * P:(j % 4) * P + n]


def banks(ps):
    return [(slice(0, 4), ps[:, 0, 0:4 * P].rearrange("p (j n) -> p j n", j=4)),
            (slice(4, 7), ps[:, 1, 0:3 * P].rearrange("p (j n) -> p j n", j=3))]


def to_attention(nc, k, table, x, att_table, a2_table, rest_table):
    ph = Phase(nc)
    norm = Norm(ph)
    WT = 2 * D + 2 * H
    own, xb = ph.sb("own", [P, 2, NBLK, D], F32), ph.sb("xb", [P, 2, NBLK, D], F32)
    xn, xT = ph.sb("xn", [P, NBLK, D], F32), ph.sb("xT", [P, NBLK, D], F32)
    rest = ph.sb("rest", [P, NBLK, D], F32)
    tl, yb = ph.sb("tl", [P, 2, NBLK, AW], F32), ph.sb("yb", [P, 2, NBLK, D], F32)
    turned = ph.ps("turned", [P, 2, 512])
    prod = [ph.ps(f"prod{j}", [P, 512]) for j in range(4)]
    loaded, stored = [ph.sem("loaded0"), ph.sem("loaded1")], [ph.sem("stored0"), ph.sem("stored1")]
    chain, xn_ready, turned_ready = ph.sem("chain"), ph.sem("xn_ready"), ph.sem("turned_ready")
    xT_ready, prod_ready = ph.sem("xT_ready"), ph.sem("prod_ready")
    copied, taken, settled = ph.sem("copied"), ph.sem("taken"), ph.sem("settled")
    with nc.Block() as block:
        @block.sync
        def _(sp):
            for i in rounds(sp, NR // 2):
                for r in range(2):
                    b = ds((i * 2 + r) * NBLK, NBLK)
                    if later(i):
                        sp.wait_ge(stored[r], i * 48)
                    sp.dma_start(own[:, r], blocks_of(table)[:, b, :]).then_inc(loaded[r], 16)
                    sp.dma_start(xb[:, r], blocks_of(x)[:, b, :]).then_inc(loaded[r], 16)

        @block.gpsimd
        def _(pool):
            for i in rounds(pool, NR // 2):
                for r in range(2):
                    b = ds((i * 2 + r) * NBLK, NBLK)
                    pool.wait_ge(copied, (i * 2 + r + 1) * NBLK)
                    pool.sem_inc(settled, 1)
                    pool.dma_start(blocks_of(att_table)[:, b, :], tl[:, r]).then_inc(stored[r], 16)
                    pool.dma_start(blocks_of(a2_table)[:, b, :], tl[:, r, :, D:AW]).then_inc(stored[r], 16)
                    pool.wait_ge(taken, (i * 2 + r + 1) * NBLK + 4)
                    pool.sem_inc(settled, 1)
                    pool.dma_start(blocks_of(rest_table)[:, b, :], yb[:, r]).then_inc(stored[r], 16)
            for r in range(2):
                pool.wait_ge(stored[r], NR // 2 * 48)

        @block.scalar
        def _(act):
            for i in rounds(act, NR // 2):
                for r in range(2):
                    R = i * 2 + r
                    norm.root(act, R + 1)
                    act.wait_ge(turned_ready, R + 1)
                    if later(i) or r > 0:
                        act.wait_ge(prod_ready, R * NBLK)
                    for sl, ps in banks(turned):
                        ins = act.copy(xT[:, sl, :], ps)
                    ins.then_inc(xT_ready, 1)
                    if later(i):
                        act.wait_ge(stored[r], i * 48)
                    for j in range(NBLK):
                        act.wait_ge(prod_ready, R * NBLK + j + 1)
                        act.copy(tl[:, r, j, :], prod[j % 4][:, 0:AW]).then_inc(copied, 1)

        @block.tensor
        def _(pe):
            for i in rounds(pe, NR // 2):
                for r in range(2):
                    R = i * 2 + r
                    pe.wait_ge(xn_ready, R + 1)
                    if later(i) or r > 0:
                        pe.wait_ge(xT_ready, R)
                    for j in range(NBLK):
                        ins = pe.transpose(bank(turned, j), xn[:, j, :], k.ident[:, :])
                    ins.then_inc(turned_ready, 1)
                    pe.wait_ge(xT_ready, R + 1)
                    for j in range(NBLK):
                        pe.wait_ge(taken, R * NBLK + j + 1)
                        if j >= 4:
                            pe.wait_ge(copied, R * NBLK + j - 3)
                        elif later(i) or r > 0:
                            pe.wait_ge(copied, R * NBLK)
                        pe.matmul(prod[j % 4][:, 0:WT], xT[:, j, :], k.w_att[:, :], start=True, stop=True)\
                          .then_inc(prod_ready, 1)

        @block.vector
        def _(dve):
            link = Chain(dve, chain)
            dve.sem_inc(taken, 4)
            for i in rounds(dve, NR // 2):
                for r in range(2):
                    R = i * 2 + r
                    first = R * NBLK
                    link.round(R, 7)
                    dve.wait_ge(loaded[r], i * 32 + 32)
                    if later(i):
                        dve.wait_ge(stored[r], i * 48)
                    link(dve.tensor_tensor(own[:, r], own[:, r], k.acc[:, ds(first, NBLK), 0:D], ALU.add))
                    for j in range(NBLK):
                        ins = dve.scalar_tensor_tensor(xb[:, r, j], own[:, r, j], k.dis[:, ds(first + j, 1)],
                                                       xb[:, r, j], ALU.mult, ALU.add)
                    link(ins)
                    norm(dve, link, xb[:, r], xn, R + 1)
                    dve.nop().then_inc(xn_ready, 1)
                    link(dve.tensor_tensor(rest[:, :, :], xn[:, :, :], bc(k.b_att[:, :], 1, NBLK), ALU.add))
                    for j in range(NBLK):
                        dve.wait_ge(copied, R * NBLK + j + 1)
                        dve.sem_inc(norm.settled, 1)
                        dve.tensor_copy(k.state[:, ds(first + j, 1), H:2 * H], prod[j % 4][:, D + H:D + 2 * H].unsqueeze(1))
                        dve.tensor_tensor(yb[:, r, j, :], rest[:, j, :], prod[j % 4][:, D + 2 * H:WT], ALU.add)\
                           .then_inc(taken, 1)
    ph.end()



def tile_blocks(nc, k, s, engine, tiles):
    _, blocks = nc.values_load_multi_w_load_instructions(
        k.tile_block[s][0:1, tiles], engines=[engine], min_val=0, max_val=NB - 1,
        skip_runtime_bounds_check_because="they are clamped to 0 .. NB - 1 where they are made")
    return blocks


def hop(nc, k, table, attributes, sums, nxt):
    ph = Phase(nc)
    W = 2 * D if attributes is not None else D
    rows = ph.sb("rows", [P, RING * B, W], F32)
    onehot = ph.sb("onehot", [P, RING * B, P], F32)
    stage = ph.sb("stage", [P, RING * B], I32)
    own, gb = ph.sb("own", [P, 2, NBLK, D], F32), ph.sb("gb", [P, 2, NBLK, D], F32)
    part = [ph.ps(f"part{j}", [P, 512]) for j in range(B)]
    zeroed, staged, chain = ph.sem("zeroed"), ph.sem("staged"), ph.sem("chain")
    gathered = [ph.sem(f"gathered{u}") for u in range(RING * B)]
    attr_in = [ph.sem(f"attr_in{r}") for r in range(RING)]
    hot, multiplied, added = ph.sem("hot"), ph.sem("multiplied"), ph.sem("added")
    own_in, stored = [ph.sem("own_in0"), ph.sem("own_in1")], [ph.sem("stored0"), ph.sem("stored1")]
    made, settled, sums_out = ph.sem("made"), ph.sem("settled"), ph.sem("sums_out")
    nodes_in = ph.sem("nodes_in")

    with nc.Block() as block:
        @block.sync
        def _(sp):
            if attributes is not None:
                with sp.Fori(0, TP // (RING * B)) as i:
                    for r in range(RING):
                        s = i * RING + r
                        sp.wait_ge(multiplied, s * B + B)
                        sp.dma_start(rows[:, r * B:(r + 1) * B, D:2 * D],
                                     attributes.rearrange("(t p) w -> p t w", p=P)[:, ds(s * B, B), 0:D])\
                          .then_inc(attr_in[r], 16)
                sp.wait_ge(added, B + TP)
                sp.dma_start(blocks_of(sums), k.acc2[:, :, :]).then_inc(sums_out, 16)
            if nxt is not None:
                for i in rounds(sp, NR // 2):
                    for r in range(2):
                        if later(i):
                            sp.wait_ge(stored[r], i * 16)
                        sp.dma_start(own[:, r], blocks_of(table)[:, ds((i * 2 + r) * NBLK, NBLK), :])\
                          .then_inc(own_in[r], 16)
            if attributes is not None:
                sp.wait_ge(sums_out, 16)

        @block.scalar
        def _(act):
            if attributes is not None:
                act.dma_start(k.nodes[1][:, 0:TP, :], k.by_dst.rearrange("(t p) w -> p t w", p=P)[:, :, DE:DE + 2])\
                   .then_inc(nodes_in, 16)
            with act.Fori(0, TP // (RING * B)) as i:
                for r in range(RING):
                    s = i * RING + r
                    act.wait_ge(multiplied, s * B + B)
                    act.copy(stage[:, r * B:(r + 1) * B], k.nodes[0][:, ds(s * B, B), 1].bitcast(I32))\
                       .then_inc(staged, 1)
            if attributes is not None:
                act.wait_ge(nodes_in, 16)
            if nxt is not None:
                with act.Fori(0, NR // 2) as i:
                    for r in range(2):
                        act.wait_ge(made, i * 2 + r + 1)
                        act.dma_start(blocks_of(nxt)[:, ds((i * 2 + r) * NBLK, NBLK), :], gb[:, r])\
                           .then_inc(stored[r], 16)
                for r in range(2):
                    act.wait_ge(stored[r], NR // 2 * 16)

        @block.gpsimd
        def _(pool):
            with pool.Fori(0, TP // (RING * B)) as i:
                for r in range(RING):
                    s = i * RING + r
                    pool.wait_ge(staged, s + 1)
                    pool.sem_inc(settled, 1)
                    for u in range(r * B, (r + 1) * B):
                        pool.indirect_dma_start(
                            out=rows[:, u, 0:D], out_offset=None, in_=table,
                            in_offset=bass.IndirectOffsetOnAxis(ap=stage[:, u:u + 1], axis=0)).then_inc(gathered[u], 16)

        @block.tensor
        def _(pe):
            pe.sem_inc(multiplied, RING * B)
            with pe.Fori(0, TP // (RING * B)) as i:
                for u in range(RING * B):
                    n = i * (RING * B) + u
                    if u % B == 0 and attributes is not None:
                        pe.wait_ge(attr_in[u // B], i * 16 + 16)
                    pe.wait_ge(hot, n + 1)
                    pe.wait_ge(gathered[u], i * 16 + 16)
                    pe.wait_ge(added, n + 1)
                    pe.matmul(part[u % B][:, 0:W], onehot[:, u, :], rows[:, u, :], start=True, stop=True)\
                      .then_inc(multiplied, 1)

        @block.vector
        def _(dve):
            def make_hot(n, u):
                dve.wait_ge(multiplied, n + 1)
                dve.tensor_scalar(onehot[:, u % (RING * B), :], k.lanes[:, :], k.nodes[0][:, ds(n, 1), 0], None,
                                  ALU.is_equal).then_inc(hot, 1)

            dve.memset(k.acc[:, :, :], 0.0).then_inc(zeroed, 1)
            if attributes is not None:
                dve.memset(k.acc2[:, :, :], 0.0).then_inc(zeroed, 1)
            dve.wait_ge(zeroed, 2 if attributes is not None else 1)
            dve.sem_inc(added, B)
            for u in range(B):
                make_hot(u, u)
            with dve.Fori(0, TP // (RING * B)) as i:
                for r in range(RING):
                    at = tile_blocks(nc, k, 0, DVE, ds(i * (RING * B) + r * B, B))
                    for v in range(B):
                        u = r * B + v
                        n = i * (RING * B) + u
                        make_hot(n + B, u + B)
                        dve.wait_ge(multiplied, n + 1 + RING * B)
                        dve.wait_ge(added, n + B)
                        if attributes is not None:
                            dve.tensor_tensor(k.acc2[:, ds(at[v], 1), :], k.acc2[:, ds(at[v], 1), :],
                                              part[v][:, D:2 * D].unsqueeze(1), ALU.add)
                        dve.tensor_tensor(k.acc[:, ds(at[v], 1), 0:D], k.acc[:, ds(at[v], 1), 0:D],
                                          part[v][:, 0:D].unsqueeze(1), ALU.add).then_inc(added, 1)
            dve.wait_ge(added, B + TP)
            if nxt is not None:
                for i in rounds(dve, NR // 2):
                    for r in range(2):
                        first = (i * 2 + r) * NBLK
                        dve.wait_ge(own_in[r], i * 16 + 16)
                        if later(i):
                            dve.wait_ge(stored[r], i * 16)
                        dve.tensor_tensor(own[:, r], own[:, r], k.acc[:, ds(first, NBLK), 0:D], ALU.add)\
                           .then_inc(chain, 1)
                        dve.wait_ge(chain, i * 2 + r + 1)
                        for j in range(NBLK):
                            ins = dve.tensor_scalar(gb[:, r, j], own[:, r, j], k.dis2[:, ds(first + j, 1)], None,
                                                    ALU.mult)
                        ins.then_inc(made, 1)
    ph.end()


def greatest(nc, k, a2_table):
    ph = Phase(nc)
    rows = ph.sb("rows", [P, RING * B, H], F32)
    onehot = ph.sb("onehot", [P, RING * B, P], F32)
    apart = ph.sb("apart", [P, B, P], F32)
    mask = ph.sb("mask", [P, 2 * B, P], F32)
    junk = ph.sb("junk", [P, 2 * H, P], F32)
    stage = ph.sb("stage", [P, RING * B], I32)
    best = ph.sb("best", [P, B, H], F32)
    total = ph.sb("total", [P, NB, H], F32)
    turned = ph.ps("turned", [P, B, P])
    values = [ph.ps(f"values{j}", [P, H, P]) for j in range(B)]
    zeroed, staged, settled = ph.sem("zeroed"), ph.sem("staged"), ph.sem("settled")
    gathered = [ph.sem(f"gathered{u}") for u in range(RING * B)]
    hot, turned_ready, mask_ready = ph.sem("hot"), ph.sem("turned_ready"), ph.sem("mask_ready")
    values_ready, values_used, raised = ph.sem("values_ready"), ph.sem("values_used"), ph.sem("raised")
    summed, apart_ready = ph.sem("summed"), ph.sem("apart_ready")
    ROUNDS = TP // (RING * B)

    with nc.Block() as block:
        @block.scalar
        def _(act):
            def put_indices(s, r):
                act.wait_ge(values_ready, s * B + B)
                act.copy(stage[:, r * B:(r + 1) * B], k.nodes[0][:, ds(s * B, B), 1].bitcast(I32))\
                   .then_inc(staged, 1)

            def turn(s, r):
                act.wait_ge(turned_ready, s + 1)
                act.wait_ge(values_used, s * B + B)
                act.activation(mask[:, r % 2 * B:r % 2 * B + B, :], turned[:, :, :], ACT.Copy, scale=FAR, bias=-FAR)\
                   .then_inc(mask_ready, 1)

            def make_hot(s, r):
                act.wait_ge(values_ready, s * B + B)
                for v in range(B):
                    ins = act.activation(apart[:, v, :], k.lanes[:, :], ACT.Abs, scale=-1.0,
                                         bias=k.nodes[0][:, ds(s * B + v, 1), 0])
                ins.then_inc(apart_ready, 1)
                act.wait_ge(apart_ready, s + 1)
                act.activation(onehot[:, r % RING * B:(r % RING + 1) * B, :], apart[:, :, :], ACT.Relu,
                               scale=-1.0, bias=1.0).then_inc(hot, 1)

            for s in range(RING - 1):
                put_indices(s, s)
            make_hot(0, 0)
            turn(0, 0)
            make_hot(1, 1)
            with act.Fori(0, ROUNDS) as i:
                for r in range(RING):
                    s = i * RING + r
                    turn(s + 1, r + 1)
                    make_hot(s + 2, r + 2)
                    put_indices(s + RING - 1, (r + RING - 1) % RING)

        @block.gpsimd
        def _(pool):
            with pool.Fori(0, ROUNDS) as i:
                for r in range(RING):
                    pool.wait_ge(staged, i * RING + r + 1)
                    pool.sem_inc(settled, 1)
                    for u in range(r * B, (r + 1) * B):
                        pool.indirect_dma_start(
                            out=rows[:, u, :], out_offset=None, in_=a2_table,
                            in_offset=bass.IndirectOffsetOnAxis(ap=stage[:, u:u + 1], axis=0)).then_inc(gathered[u], 16)

        @block.tensor
        def _(pe):
            def turn(s, r):
                pe.wait_ge(hot, s + 1)
                pe.wait_ge(mask_ready, s + 1)
                for v in range(B):
                    ins = pe.transpose(turned[:, v, :], onehot[:, r % RING * B + v, :], k.ident[:, :])
                ins.then_inc(turned_ready, 1)

            pe.sem_inc(values_ready, RING * B)
            turn(0, 0)
            with pe.Fori(0, ROUNDS) as i:
                for r in range(RING):
                    s = i * RING + r
                    for v in range(B):
                        pe.wait_ge(gathered[r * B + v], i * 16 + 16)
                        pe.wait_ge(values_used, (s + 1) * B + v + 1)
                        for q in range(H):
                            ins = pe.matmul(values[v][:, q, :], rows[:, r * B + v, q:q + 1].to_broadcast([P, P]),
                                            k.ident[:, :], start=True, stop=True)
                        ins.then_inc(values_ready, 1)
                        if v == 0:
                            turn(s + 1, r + 1)

        @block.vector
        def _(dve):
            def raise_to(n, v, b):
                dve.wait_ge(values_used, n + 1 + 2 * B)
                dve.wait_ge(raised, n + B)
                dve.tensor_tensor(k.state[:, ds(b, 1), 0:H], k.state[:, ds(b, 1), 0:H], best[:, v:v + 1, :],
                                  ALU.max).then_inc(raised, 1)

            dve.memset(k.state[:, :, 0:H], -FAR).then_inc(zeroed, 1)
            dve.wait_ge(zeroed, 1)
            dve.sem_inc(mask_ready, 1)
            dve.sem_inc(values_used, 2 * B)
            dve.sem_inc(raised, B)
            for i in rounds(dve, ROUNDS):
                for r in range(RING):
                    s = i * RING + r
                    behind = later(i) or r > 0
                    dve.wait_ge(mask_ready, s + 2)
                    for v in range(B):
                        n = s * B + v
                        if v == 0 or (v == 1 and not behind):
                            dve.wait_ge(values_ready, n + 1 + RING * B)
                            dve.sem_inc(settled, 1)
                        for q in range(H):
                            ins = dve.tensor_tensor_reduce(junk[:, v % 2 * H + q, :], values[v][:, q, :],
                                                           mask[:, r % 2 * B + v, :], 1.0, -FAR, ALU.add, ALU.max,
                                                           best[:, v, q:q + 1])
                        ins.then_inc(values_used, 1)
                        if v == 0 and behind:
                            at = tile_blocks(nc, k, 0, DVE, ds(s * B - 1, B + 1))
                            last, at = at[0], at[1:]
                        elif v == 0:
                            at = tile_blocks(nc, k, 0, DVE, slice(0, B))
                        if v < B - 1 and (v > 0 or behind):
                            dve.wait_ge(values_ready, n + 2 + RING * B)
                        if v > 0:
                            raise_to(n - 1, v - 1, at[v - 1])
                        elif behind:
                            raise_to(n - 1, B - 1, last)
            raise_to(TP - 1, B - 1, tile_blocks(nc, k, 0, DVE, slice(TP - 1, TP))[0])
            dve.wait_ge(raised, TP + B)
            dve.tensor_tensor(total[:, :, :], k.state[:, :, 0:H], k.state[:, :, H:2 * H], ALU.add).then_inc(summed, 1)
            dve.wait_ge(summed, 1)
            dve.scalar_tensor_tensor(k.state[:, :, 0:H], total[:, :, :], 0.2, total[:, :, :], ALU.mult, ALU.max)
    ph.end()


def attention(nc, k, att_table):
    ph = Phase(nc)
    rows = ph.sb("rows", [P, RING * B, AW], F32)
    onehot = ph.sb("onehot", [P, RING * B, P], F32)
    weighed = ph.sb("weighed", [P, 2 * B, H, HD + 1], F32)
    turned_sb = ph.sb("turned_sb", [P, 2 * B, P], F32)
    stage = ph.sb("stage", [P, RING * B], I32)
    score = ph.sb("score", [P, 2 * B, H], F32)
    turned = ph.ps("turned", [P, B, P])
    looked = [ph.ps(f"looked{j}", [P, B, 2 * H]) for j in range(2)]
    part = [ph.ps(f"part{j}", [P, 512]) for j in range(B)]
    zeroed, staged, chain = ph.sem("zeroed"), ph.sem("staged"), ph.sem("chain")
    gathered = [ph.sem(f"gathered{u}") for u in range(RING * B)]
    used, hot, turned_ready, copied = ph.sem("used"), ph.sem("hot"), ph.sem("turned_ready"), ph.sem("copied")
    looked_ready, score_ready, weight_ready = ph.sem("looked_ready"), ph.sem("score_ready"), ph.sem("weight_ready")
    weighed_ready, added, settled = ph.sem("weighed_ready"), ph.sem("added"), ph.sem("settled")
    ROUNDS = TP // (RING * B)

    with nc.Block() as block:
        @block.scalar
        def _(act):
            def put_indices(s, r):
                act.wait_ge(used, s * B + B)
                act.copy(stage[:, r * B:(r + 1) * B], k.nodes[0][:, ds(s * B, B), 1].bitcast(I32))\
                   .then_inc(staged, 1)

            def turn(s, r):
                act.wait_ge(turned_ready, s + 1)
                act.copy(turned_sb[:, r % 2 * B:r % 2 * B + B, :], turned[:, :, :]).then_inc(copied, 1)

            for s in range(RING - 1):
                put_indices(s, s)
            turn(0, 0)
            with act.Fori(0, ROUNDS) as i:
                for r in range(RING):
                    s = i * RING + r
                    b = slice(r % 2 * B, r % 2 * B + B)
                    act.wait_ge(score_ready, s + 3)
                    act.activation(weighed[:, b, :, HD], score[:, b, :], ACT.Exp).then_inc(weight_ready, 1)
                    turn(s + 1, r + 1)
                    put_indices(s + RING - 1, (r + RING - 1) % RING)

        @block.gpsimd
        def _(pool):
            with pool.Fori(0, ROUNDS) as i:
                for r in range(RING):
                    pool.wait_ge(staged, i * RING + r + 1)
                    pool.sem_inc(settled, 1)
                    for u in range(r * B, (r + 1) * B):
                        pool.indirect_dma_start(
                            out=rows[:, u, :], out_offset=None, in_=att_table,
                            in_offset=bass.IndirectOffsetOnAxis(ap=stage[:, u:u + 1], axis=0)).then_inc(gathered[u], 16)

        @block.tensor
        def _(pe):
            def turn(s, r):
                pe.wait_ge(hot, s + 1)
                for v in range(B):
                    ins = pe.transpose(turned[:, v, :], onehot[:, r % RING * B + v, :], k.ident[:, :])
                ins.then_inc(turned_ready, 1)

            def sum_up(s, r):
                pe.wait_ge(weighed_ready, s + 1)
                for v in range(B):
                    pe.wait_ge(added, s * B + v + 1)
                    pe.matmul(part[v][:, 0:AW], onehot[:, r % RING * B + v, :],
                              weighed[:, r % 2 * B + v, :, :].rearrange("p a b -> p (a b)"), start=True, stop=True)\
                      .then_inc(used, 1)

            pe.sem_inc(used, RING * B)
            turn(0, 0)
            for i in rounds(pe, ROUNDS):
                for r in range(RING):
                    s = i * RING + r
                    at = tile_blocks(nc, k, 0, mybir.EngineType.PE, ds(s * B, B))
                    pe.wait_ge(copied, s + 1)
                    pe.wait_ge(score_ready, s + 1)
                    for v in range(B):
                        ins = pe.matmul(looked[r % 2][:, v, :], turned_sb[:, r % 2 * B + v, :],
                                        k.state[:, ds(at[v], 1), :].rearrange("p o h -> p (o h)"),
                                        start=True, stop=True)
                    ins.then_inc(looked_ready, 1)
                    turn(s + 1, r + 1)
                    if later(i) or r > 0:
                        sum_up(s - 1, r + RING - 1)
            sum_up(ROUNDS * RING - 1, RING - 1)

        @block.vector
        def _(dve):
            link = Chain(dve, chain)

            def make_hot(s, r):
                dve.wait_ge(used, s * B + B)
                dve.tensor_tensor(onehot[:, r % RING * B:(r % RING + 1) * B, :], bc(k.lanes[:, :], 1, B),
                                  k.nodes[0][:, ds(s * B, B), 0:1].to_broadcast([P, B, P]), ALU.is_equal)\
                   .then_inc(hot, 1)

            def sum_up(s, at):
                for v in range(B):
                    n = s * B + v
                    dve.wait_ge(added, n + B)
                    dve.wait_ge(used, n + 1 + RING * B)
                    dve.tensor_tensor(k.acc[:, ds(at[v], 1), :], k.acc[:, ds(at[v], 1), :],
                                      part[v][:, 0:AW].unsqueeze(1), ALU.add).then_inc(added, 1)

            dve.memset(k.acc[:, :, :], 0.0).then_inc(zeroed, 1)
            dve.wait_ge(zeroed, 1)
            dve.sem_inc(score_ready, 2)
            dve.sem_inc(added, B)
            make_hot(0, 0)
            make_hot(1, 1)
            for i in rounds(dve, ROUNDS):
                for r in range(RING):
                    s = i * RING + r
                    b = slice(r % 2 * B, r % 2 * B + B)
                    link.round(s, 3)
                    dve.wait_ge(looked_ready, s + 1)
                    for u in range(r * B, (r + 1) * B):
                        dve.wait_ge(gathered[u], i * 16 + 16)
                    link(dve.tensor_tensor(score[:, b, :], looked[r % 2][:, :, H:2 * H],
                                           rows[:, r * B:(r + 1) * B, D:AW], ALU.add))
                    link(dve.scalar_tensor_tensor(score[:, b, :], score[:, b, :], 0.2, score[:, b, :],
                                                  ALU.mult, ALU.max))
                    link(dve.tensor_tensor(score[:, b, :], score[:, b, :], looked[r % 2][:, :, 0:H], ALU.subtract))
                    dve.tensor_scalar(score[:, b, :], score[:, b, :], 0.0, None, ALU.min).then_inc(score_ready, 1)
                    make_hot(s + 2, r + 2)
                    if later(i) or r > 0:
                        sum_up(s - 1, tile_blocks(nc, k, 0, DVE, ds((s - 1) * B, B)))
                    dve.wait_ge(weight_ready, s + 1)
                    dve.tensor_tensor(weighed[:, b, :, 0:HD],
                                      rows[:, r * B:(r + 1) * B, 0:D].rearrange("p t (a b) -> p t a b", a=H),
                                      weighed[:, b, :, HD:HD + 1].to_broadcast([P, B, H, HD]), ALU.mult)\
                       .then_inc(weighed_ready, 1)
            sum_up(ROUNDS * RING - 1, tile_blocks(nc, k, 0, DVE, slice(TP - B, TP)))
    ph.end()


def to_messages(nc, k, rest_table, x2_table, p_table):
    ph = Phase(nc)
    norm = Norm(ph)
    xb = ph.sb("xb", [P, 2, NBLK, D], F32)
    msg, inv = ph.sb("msg", [P, NBLK, D], F32), ph.sb("inv", [P, NBLK, H], F32)
    xn, xT = ph.sb("xn", [P, 2, NBLK, D], F32), ph.sb("xT", [P, NBLK, D], F32)
    pb = ph.sb("pb", [P, 2, NBLK, D], F32)
    turned = ph.ps("turned", [P, 2, 512])
    prod = [ph.ps(f"prod{j}", [P, 512]) for j in range(4)]
    loaded, stored = [ph.sem("loaded0"), ph.sem("loaded1")], [ph.sem("stored0"), ph.sem("stored1")]
    chain, xn_ready, turned_ready = ph.sem("chain"), ph.sem("xn_ready"), ph.sem("turned_ready")
    xT_ready, prod_ready, settled = ph.sem("xT_ready"), ph.sem("prod_ready"), ph.sem("settled")
    copied, taken = ph.sem("copied"), ph.sem("taken")
    with nc.Block() as block:
        @block.sync
        def _(sp):
            for i in rounds(sp, NR // 2):
                for r in range(2):
                    if later(i):
                        sp.wait_ge(stored[r], i * 32)
                    sp.dma_start(xb[:, r], blocks_of(rest_table)[:, ds((i * 2 + r) * NBLK, NBLK), :])\
                      .then_inc(loaded[r], 16)

        @block.gpsimd
        def _(pool):
            for i in rounds(pool, NR // 2):
                for r in range(2):
                    b = ds((i * 2 + r) * NBLK, NBLK)
                    pool.wait_ge(xn_ready, i * 2 + r + 1)
                    pool.sem_inc(settled, 1)
                    pool.dma_start(blocks_of(x2_table)[:, b, :], xn[:, r]).then_inc(stored[r], 16)
                    pool.wait_ge(copied, (i * 2 + r + 1) * NBLK)
                    pool.sem_inc(settled, 1)
                    pool.dma_start(blocks_of(p_table)[:, b, :], pb[:, r]).then_inc(stored[r], 16)
            for r in range(2):
                pool.wait_ge(stored[r], NR // 2 * 32)

        @block.scalar
        def _(act):
            for i in rounds(act, NR // 2):
                for r in range(2):
                    R = i * 2 + r
                    norm.root(act, R + 1)
                    act.wait_ge(turned_ready, R + 1)
                    if later(i) or r > 0:
                        act.wait_ge(prod_ready, R * NBLK)
                    for sl, ps in banks(turned):
                        ins = act.copy(xT[:, sl, :], ps)
                    ins.then_inc(xT_ready, 1)
                    if later(i):
                        act.wait_ge(stored[r], i * 32)
                    for j in range(NBLK):
                        act.wait_ge(prod_ready, R * NBLK + j + 1)
                        act.copy(pb[:, r, j, :], prod[j % 4][:, 0:D]).then_inc(copied, 1)

        @block.tensor
        def _(pe):
            for i in rounds(pe, NR // 2):
                for r in range(2):
                    R = i * 2 + r
                    pe.wait_ge(xn_ready, R + 1)
                    if later(i) or r > 0:
                        pe.wait_ge(xT_ready, R)
                    for j in range(NBLK):
                        ins = pe.transpose(bank(turned, j), xn[:, r, j, :], k.ident[:, :])
                    ins.then_inc(turned_ready, 1)
                    pe.wait_ge(xT_ready, R + 1)
                    for j in range(NBLK):
                        pe.wait_ge(taken, R * NBLK + j + 1)
                        if later(i) or r > 0 or j >= 4:
                            pe.wait_ge(copied, R * NBLK + (j - 3 if j >= 4 else 0))
                        pe.matmul(prod[j % 4][:, 0:2 * D], xT[:, j, :], k.w_msg[:, :], start=True, stop=True)\
                          .then_inc(prod_ready, 1)

        @block.vector
        def _(dve):
            link = Chain(dve, chain)
            dve.sem_inc(taken, 4)
            for i in rounds(dve, NR // 2):
                for r in range(2):
                    R = i * 2 + r
                    first = R * NBLK
                    sums = k.acc[:, ds(first, NBLK), :].rearrange("p n (a b) -> p n a b", a=H)
                    link.round(R, 8)
                    dve.wait_ge(loaded[r], i * 16 + 16)
                    if later(i):
                        dve.wait_ge(stored[r], i * 32)
                    link(dve.tensor_scalar(inv[:, :, :], sums[:, :, :, HD], 0.5, None, ALU.max))
                    link(dve.reciprocal(inv[:, :, :], inv[:, :, :]))
                    for j in range(NBLK):
                        ins = dve.tensor_tensor(msg[:, j, :].rearrange("p (a b) -> p a b", a=H),
                                                k.acc[:, ds(first + j, 1), :].rearrange("p o (a b) -> p (o a) b", a=H)[:, :, 0:HD],
                                                inv[:, j, :].unsqueeze(2).to_broadcast([P, H, HD]), ALU.mult)
                    link(ins)
                    link(dve.tensor_tensor(xb[:, r], xb[:, r], msg[:, :, :], ALU.add))
                    norm(dve, link, xb[:, r], xn[:, r], R + 1)
                    dve.nop().then_inc(xn_ready, 1)
                    for j in range(NBLK):
                        dve.wait_ge(copied, R * NBLK + j + 1)
                        dve.sem_inc(norm.settled, 1)
                        dve.tensor_tensor(k.acc2[:, ds(first + j, 1), :], prod[j % 4][:, D:2 * D].unsqueeze(1),
                                          k.b_msg[:, :].unsqueeze(1), ALU.add)\
                           .then_inc(taken, 1)
    ph.end()


def messages(nc, k, p_table):
    ph = Phase(nc)
    rows = ph.sb("rows", [P, RING * B, D], F32)
    attr, attr_t = ph.sb("attr", [P, RING * B, DE], F32), ph.sb("attr_t", [DE, 2 * B, P], F32)
    onehot, turned_sb = ph.sb("onehot", [P, RING * B, P], F32), ph.sb("turned_sb", [P, 2 * B, P], F32)
    pre, hid = ph.sb("pre", [P, 2 * B, D], F32), ph.sb("hid", [P, 2 * B, D + 1], F32)
    stage = ph.sb("stage", [P, RING * B], I32)
    turned, attr_turned = ph.ps("turned", [P, B, P]), ph.ps("attr_turned", [DE, B, P])
    local = [ph.ps(f"local{j}", [P, B, D]) for j in range(2)]
    part = [ph.ps(f"part{j}", [P, 512]) for j in range(B)]
    zeroed, staged, settled = ph.sem("zeroed"), ph.sem("staged"), ph.sem("settled")
    gathered = [ph.sem(f"gathered{u}") for u in range(RING * B)]
    attr_in = [ph.sem(f"attr_in{r}") for r in range(RING)]
    used, hot, turned_ready = ph.sem("used"), ph.sem("hot"), ph.sem("turned_ready")
    copied, local_ready, pre_ready = ph.sem("copied"), ph.sem("local_ready"), ph.sem("pre_ready")
    hid_ready, added = ph.sem("hid_ready"), ph.sem("added")
    ROUNDS = TP // (RING * B)

    with nc.Block() as block:
        @block.sync
        def _(sp):
            def load(s, r, of):
                sp.wait_ge(used, s * B + B)
                sp.dma_start(attr[:, r * B:(r + 1) * B, :],
                             k.by_dst.rearrange("(t p) w -> p t w", p=P)[:, of, 0:DE]).then_inc(attr_in[r], 16)

            with sp.Fori(0, ROUNDS) as i:
                for r in range(RING):
                    load(i * RING + r, r, ds((i * RING + r) * B, B))
            load(ROUNDS * RING, 0, slice(0, B))

        @block.scalar
        def _(act):
            def put_indices(s, r):
                act.wait_ge(used, s * B + B)
                act.copy(stage[:, r * B:(r + 1) * B], k.nodes[1][:, ds(s * B, B), 1].bitcast(I32))\
                   .then_inc(staged, 1)

            def turn(s, r):
                b = slice(r % 2 * B, r % 2 * B + B)
                act.wait_ge(turned_ready, s + 1)
                act.copy(turned_sb[:, b, :], turned[:, :, :])
                act.copy(attr_t[:, b, :], attr_turned[:, :, :]).then_inc(copied, 1)

            act.wait_ge(zeroed, 2)
            for s in range(RING - 1):
                put_indices(s, s)
            turn(0, 0)
            with act.Fori(0, ROUNDS) as i:
                for r in range(RING):
                    s = i * RING + r
                    b = slice(r % 2 * B, r % 2 * B + B)
                    turn(s + 1, r + 1)
                    act.wait_ge(pre_ready, s + 3)
                    act.activation(hid[:, b, 0:D], pre[:, b, :], ACT.Relu).then_inc(hid_ready, 1)
                    put_indices(s + RING - 1, (r + RING - 1) % RING)

        @block.gpsimd
        def _(pool):
            with pool.Fori(0, ROUNDS) as i:
                for r in range(RING):
                    pool.wait_ge(staged, i * RING + r + 1)
                    pool.sem_inc(settled, 1)
                    for u in range(r * B, (r + 1) * B):
                        pool.indirect_dma_start(
                            out=rows[:, u, :], out_offset=None, in_=p_table,
                            in_offset=bass.IndirectOffsetOnAxis(ap=stage[:, u:u + 1], axis=0)).then_inc(gathered[u], 16)

        @block.tensor
        def _(pe):
            def turn(s, r, nth):
                pe.wait_ge(attr_in[r % RING], nth * 16 + 16)
                pe.wait_ge(hot, s * B + B)
                for v in range(B):
                    u = r % RING * B + v
                    pe.transpose(turned[:, v, :], onehot[:, u, :], k.ident[:, :])
                    ins = pe.transpose(attr_turned[:, v, :], attr[:, u, :], k.ident[:, :])
                ins.then_inc(turned_ready, 1)

            def sum_up(s, r):
                pe.wait_ge(hid_ready, s + 1)
                for v in range(B):
                    pe.wait_ge(added, s * B + v + 1)
                    pe.matmul(part[v][:, 0:D + 1], onehot[:, r % RING * B + v, :], hid[:, r % 2 * B + v, :],
                              start=True, stop=True).then_inc(used, 1)

            pe.sem_inc(used, RING * B)
            turn(0, 0, 0)
            for i in rounds(pe, ROUNDS):
                for r in range(RING):
                    s = i * RING + r
                    at = tile_blocks(nc, k, 1, mybir.EngineType.PE, ds(s * B, B))
                    pe.wait_ge(copied, s + 1)
                    pe.wait_ge(pre_ready, s + 1)
                    for v in range(B):
                        c = r % 2 * B + v
                        pe.matmul(local[r % 2][:, v, :], turned_sb[:, c, :],
                                  k.acc2[:, ds(at[v], 1), :].rearrange("p o d -> p (o d)"), start=True, stop=False)
                        ins = pe.matmul(local[r % 2][:, v, :], attr_t[:, c, :], k.w_edge[:, :], start=False, stop=True)
                    ins.then_inc(local_ready, 1)
                    turn(s + 1, r + 1, i + (r + 1) // RING)
                    if later(i) or r > 0:
                        sum_up(s - 1, r + RING - 1)
            sum_up(ROUNDS * RING - 1, RING - 1)

        @block.vector
        def _(dve):
            def make_hot(s, r):
                dve.wait_ge(used, s * B + B)
                for v in range(B):
                    ins = dve.tensor_scalar(onehot[:, r % RING * B + v, :], k.lanes[:, :],
                                            k.nodes[1][:, ds(s * B + v, 1), 0], None, ALU.is_equal)
                    ins.then_inc(hot, 1)

            def sum_up(s, at):
                for v in range(B):
                    n = s * B + v
                    dve.wait_ge(used, n + 1 + RING * B)
                    dve.wait_ge(added, n + B)
                    dve.tensor_tensor(k.acc[:, ds(at[v], 1), 0:D + 1], k.acc[:, ds(at[v], 1), 0:D + 1],
                                      part[v][:, 0:D + 1].unsqueeze(1), ALU.add).then_inc(added, 1)

            dve.memset(k.acc[:, :, :], 0.0).then_inc(zeroed, 1)
            dve.memset(hid[:, :, D:D + 1], 1.0).then_inc(zeroed, 1)
            dve.wait_ge(zeroed, 2)
            dve.sem_inc(pre_ready, 2)
            dve.sem_inc(added, B)
            make_hot(0, 0)
            for i in rounds(dve, ROUNDS):
                for r in range(RING):
                    s = i * RING + r
                    b = slice(r % 2 * B, r % 2 * B + B)
                    make_hot(s + 1, r + 1)
                    dve.wait_ge(local_ready, s + 1)
                    for u in range(r * B, (r + 1) * B):
                        dve.wait_ge(gathered[u], i * 16 + 16)
                    dve.tensor_tensor(pre[:, b, :], rows[:, r * B:(r + 1) * B, :], local[r % 2][:, :, :], ALU.add)\
                       .then_inc(pre_ready, 1)
                    if later(i) or r > 0:
                        sum_up(s - 1, tile_blocks(nc, k, 1, DVE, ds((s - 1) * B, B)))
            sum_up(ROUNDS * RING - 1, tile_blocks(nc, k, 1, DVE, slice(TP - B, TP)))
    ph.end()


HALVES = (slice(0, 4), slice(4, 7))


class Pair:

    def __init__(self, eng, sem):
        self.eng, self.sem, self.n, self.base = eng, sem, 0, 0

    def round(self, R, steps, first):
        self.base, self.n = R * (2 * steps), 0
        if not first:
            self.eng.wait_ge(self.sem, self.base)

    def behind(self, h):
        if self.n > 0:
            self.eng.wait_ge(self.sem, self.base + 2 * self.n - 1 + h)

    def __call__(self, step):
        for h, sl in enumerate(HALVES):
            self.behind(h)
            step(h, sl).then_inc(self.sem, 1)
        self.n += 1

    def announce(self, sem):
        for h in range(2):
            self.behind(h)
            self.eng.nop().then_inc(sem, 1)


class PairNorm:

    STEPS = 5

    def __init__(self, ph):
        self.stats = ph.sb("stats", [P, NBLK, 6], F32)
        self.mv = ph.sb("mv", [P, NBLK, 2], F32)
        self.var, self.std = ph.sb("var", [P, NBLK], F32), ph.sb("std", [P, NBLK], F32)
        self.rstd = ph.sb("rstd", [P, NBLK], F32)
        self.settled = ph.sem("settled_stats")
        self.var_ready, self.std_ready = ph.sem("var_ready"), ph.sem("std_ready")

    def root(self, act, use):
        for h, sl in enumerate(HALVES):
            act.wait_ge(self.var_ready, use * 2 + h + 1)
            act.activation(self.std[:, sl], self.var[:, sl], ACT.Sqrt).then_inc(self.std_ready, 1)

    def __call__(self, dve, pair, y, out, use):
        def stats(h, sl):
            for j in range(NBLK)[sl]:
                ins = dve.bn_stats(self.stats[:, j, :], y[:, j, :])
            return ins

        def moments(h, sl):
            dve.sem_inc(self.settled, 1)
            for j in range(NBLK)[sl]:
                ins = dve.bn_aggr(self.mv[:, j, :], self.stats[:, j, :])
            return ins

        def scale(h, sl):
            for j in range(NBLK)[sl]:
                ins = dve.tensor_scalar(out[:, j, :], y[:, j, :], self.mv[:, j, 0:1], self.rstd[:, j:j + 1],
                                        ALU.subtract, ALU.mult)
            return ins

        def root_of(h, sl):
            dve.wait_ge(self.std_ready, use * 2 + h + 1)
            return dve.reciprocal(self.rstd[:, sl], self.std[:, sl])

        pair(stats)
        pair(moments)
        pair(lambda h, sl: dve.tensor_scalar(self.var[:, sl], self.mv[:, sl, 1], EPS, None, ALU.add))
        pair.announce(self.var_ready)
        pair(root_of)
        pair(scale)


def half(ps, h):
    n = HALVES[h].stop - HALVES[h].start
    return ps[:, h, 0:n * P].rearrange("p (j n) -> p j n", j=n)


def finish(nc, k, x2_table, agg3, out_table, out):
    ph = Phase(nc)
    norm = PairNorm(ph)
    x2, ag = ph.sb("x2", [P, 2, NBLK, D], F32), ph.sb("ag", [P, 2, NBLK, D], F32)
    ab = ph.sb("ab", [P, NBLK, D + 1], F32)
    y, z = ph.sb("y", [P, NBLK, D], F32), ph.sb("z", [P, NBLK, D], F32)
    x3, outb = ph.sb("x3", [P, NBLK, D], F32), ph.sb("outb", [P, 2, NBLK, D], F32)
    tA, tB = ph.sb("tA", [P, NBLK, D], F32), ph.sb("tB", [P, NBLK, D], F32)
    cn = ph.sb("cn", [1, NBLK, P], F32)
    free = k.acc2[:, :, :].rearrange("p a b -> p (a b)")
    SZ = 2 * NBLK * P
    act_in, sig = (free[:, n * SZ:(n + 1) * SZ].rearrange("p (a b c) -> p a b c", a=2, b=NBLK) for n in range(2))
    bigA, bigB, bigC = ph.ps("bigA", [P, 2, 512]), ph.ps("bigB", [P, 2, 512]), ph.ps("bigC", [P, 2, 512])
    cnt_ps = ph.ps("cnt_ps", [1, 2, 512])
    loaded, stored = [ph.sem("loaded0"), ph.sem("loaded1")], [ph.sem("stored0"), ph.sem("stored1")]
    chain = ph.sem("chain")
    sums_in, turned, turned_out = ph.sem("sums_in"), ph.sem("turned"), ph.sem("turned_out")
    agg_ready, agg_out, upd_ready = ph.sem("agg_ready"), ph.sem("agg_out"), ph.sem("upd_ready")
    x3_ready, x3_turned, x3_out = ph.sem("x3_ready"), ph.sem("x3_turned"), ph.sem("x3_out")
    up_ready, up_out, hid_ready = ph.sem("up_ready"), ph.sem("up_out"), ph.sem("hid_ready")
    down_ready, down_out, out_ready = ph.sem("down_ready"), ph.sem("down_out"), ph.sem("out_ready")
    copied_out, settled = ph.sem("copied_out"), ph.sem("settled")
    both = list(enumerate(HALVES))
    with nc.Block() as block:
        @block.sync
        def _(sp):
            for i in rounds(sp, NR // 2):
                for r in range(2):
                    b = ds((i * 2 + r) * NBLK, NBLK)
                    if later(i):
                        sp.wait_ge(stored[r], i * 16)
                    sp.dma_start(x2[:, r], blocks_of(x2_table)[:, b, :]).then_inc(loaded[r], 16)
                    sp.dma_start(ag[:, r], blocks_of(agg3)[:, b, :]).then_inc(loaded[r], 16)
            for r in range(2):
                sp.wait_ge(stored[r], NR // 2 * 16)
            sp.dma_start(out, out_table[0:N, :]).then_inc(copied_out, 16)
            sp.wait_ge(copied_out, 16)

        @block.gpsimd
        def _(pool):
            for i in rounds(pool, NR // 2):
                for r in range(2):
                    pool.wait_ge(out_ready, (i * 2 + r) * 2 + 2)
                    pool.sem_inc(settled, 1)
                    pool.dma_start(blocks_of(out_table)[:, ds((i * 2 + r) * NBLK, NBLK), :], outb[:, r])\
                        .then_inc(stored[r], 16)

        @block.scalar
        def _(act):
            for i in rounds(act, NR // 2):
                for r in range(2):
                    R = i * 2 + r
                    for h, sl in both:
                        if later(i) or r > 0:
                            act.wait_ge(turned, R * 2)
                        n = sl.stop - sl.start
                        act.copy(ab[:, sl, :], k.acc[:, ds(R * NBLK + sl.start, n), 0:D + 1]).then_inc(sums_in, 1)
                    for h, sl in both:
                        act.wait_ge(turned, R * 2 + h + 1)
                        act.copy(tA[:, sl, :], half(bigA, h))
                        act.copy(cn[:, sl, :], half(cnt_ps, h)).then_inc(turned_out, 1)
                    for h, sl in both:
                        act.wait_ge(agg_ready, R * 2 + h + 1)
                        act.copy(tB[:, sl, :], half(bigB, h)).then_inc(agg_out, 1)
                    norm.root(act, R * 4)
                    norm.root(act, R * 4 + 1)
                    for h, sl in both:
                        act.wait_ge(x3_turned, R * 2 + h + 1)
                        act.copy(tA[:, sl, :], half(bigA, h))
                        act.copy(tB[:, sl, :], half(bigB, h)).then_inc(x3_out, 1)
                    for h, sl in both:
                        act.wait_ge(up_ready, R * 2 + h + 1)
                        for m, ps in enumerate((bigA, bigC)):
                            act.activation(act_in[:, m, sl, :], half(ps, h), ACT.Identity, bias=k.b_up[:, m:m + 1])
                        for m, ps in enumerate((bigA, bigC)):
                            ins = act.activation(sig[:, m, sl, :], half(ps, h), ACT.Sigmoid, bias=k.b_up[:, m:m + 1])
                        ins.then_inc(up_out, 1)
                    norm.root(act, R * 4 + 2)
                    norm.root(act, R * 4 + 3)

        @block.tensor
        def _(pe):
            for i in rounds(pe, NR // 2):
                for r in range(2):
                    R = i * 2 + r
                    for h, sl in both:
                        pe.wait_ge(sums_in, R * 2 + h + 1)
                        if later(i) or r > 0:
                            pe.wait_ge(up_out, R * 2)
                        for j in range(NBLK)[sl]:
                            pe.transpose(bank(bigA, j), ab[:, j, 0:D], k.ident[:, :])
                            ins = pe.matmul(bank(cnt_ps, j), ab[:, j, D:D + 1], k.ident[:, :], start=True, stop=True)
                        ins.then_inc(turned, 1)
                    for h, sl in both:
                        pe.wait_ge(turned_out, R * 2 + h + 1)
                        if later(i) or r > 0:
                            pe.wait_ge(down_out, R * 2)
                        for j in range(NBLK)[sl]:
                            pe.matmul(bank(bigB, j), k.w_out[:, :], tA[:, j, :], start=True, stop=False)
                            ins = pe.matmul(bank(bigB, j), k.b_out[:, :], cn[:, j, :], start=False, stop=True)
                        ins.then_inc(agg_ready, 1)
                    for h, sl in both:
                        pe.wait_ge(agg_out, R * 2 + h + 1)
                        for j in range(NBLK)[sl]:
                            pe.matmul(bank(bigC, j), tB[:, j, :], k.w_upd[:, :], start=True, stop=False)
                            ins = pe.matmul(bank(bigC, j), k.ones[0:1, :], k.b_upd[:, :], start=False, stop=True)
                        ins.then_inc(upd_ready, 1)
                    pe.wait_ge(loaded[r], i * 32 + 32)
                    for j in range(NBLK):
                        pe.transpose(bank(bigB, j), ag[:, r, j, :], k.ident[:, :])
                    for h, sl in both:
                        pe.wait_ge(x3_ready, R * 2 + h + 1)
                        for j in range(NBLK)[sl]:
                            ins = pe.transpose(bank(bigA, j), x3[:, j, :], k.ident[:, :])
                        ins.then_inc(x3_turned, 1)
                    for h, sl in both:
                        pe.wait_ge(x3_out, R * 2 + h + 1)
                        for m, ps in enumerate((bigA, bigC)):
                            for j in range(NBLK)[sl]:
                                pe.matmul(bank(ps, j), k.w_up[:, 0, m * P:(m + 1) * P], tA[:, j, :],
                                          start=True, stop=False)
                                ins = pe.matmul(bank(ps, j), k.w_up[:, 1, m * P:(m + 1) * P], tB[:, j, :],
                                                start=False, stop=True)
                        ins.then_inc(up_ready, 1)
                    for h, sl in both:
                        pe.wait_ge(hid_ready, R * 2 + h + 1)
                        for j in range(NBLK)[sl]:
                            for m in range(2):
                                pe.matmul(bank(bigB, j), act_in[:, m, j, :], k.w_down[:, m, :],
                                          start=(m == 0), stop=False)
                            ins = pe.matmul(bank(bigB, j), k.ones[0:1, :], k.b_down[:, :], start=False, stop=True)
                        ins.then_inc(down_ready, 1)

        @block.vector
        def _(dve):
            pair = Pair(dve, chain)

            def affine(t, n):
                for c, op in ((2 * n, ALU.mult), (2 * n + 1, ALU.add)):
                    pair(lambda h, sl: dve.tensor_tensor(
                        t[:, sl, :], t[:, sl, :], k.scales[:, c:c + 1, :].to_broadcast([P, sl.stop - sl.start, D]), op))

            for i in rounds(dve, NR // 2):
                for r in range(2):
                    R = i * 2 + r

                    def updated(h, sl):
                        dve.wait_ge(upd_ready, R * 2 + h + 1)
                        return dve.scalar_tensor_tensor(y[:, sl, :], half(bigC, h), 0.0, x2[:, r, sl, :],
                                                        ALU.max, ALU.add)

                    def down(h, sl):
                        dve.wait_ge(down_ready, R * 2 + h + 1)
                        return dve.tensor_scalar(y[:, sl, :], half(bigB, h), 0.0, None, ALU.add)

                    pair.round(R, 4 * norm.STEPS + 8, first=not later(i) and r == 0)
                    dve.wait_ge(loaded[r], i * 32 + 32)
                    pair(updated)
                    norm(dve, pair, y, z, R * 4)
                    affine(z, 0)
                    pair(lambda h, sl: dve.tensor_tensor(z[:, sl, :], z[:, sl, :], x2[:, r, sl, :], ALU.add))
                    norm(dve, pair, z, x3, R * 4 + 1)
                    pair.announce(x3_ready)
                    for h, sl in both:
                        dve.wait_ge(up_out, R * 2 + h + 1)
                        dve.tensor_tensor(act_in[:, :, sl, :], act_in[:, :, sl, :], sig[:, :, sl, :], ALU.mult)\
                           .then_inc(hid_ready, 1)
                    pair(down)
                    pair.announce(down_out)
                    norm(dve, pair, y, z, R * 4 + 2)
                    affine(z, 1)
                    pair(lambda h, sl: dve.scalar_tensor_tensor(y[:, sl, :], x3[:, sl, :], 2.0, z[:, sl, :],
                                                                ALU.mult, ALU.add))
                    if later(i):
                        dve.wait_ge(stored[r], i * 16)
                    norm(dve, pair, y, outb[:, r], R * 4 + 3)
                    pair.announce(out_ready)
    ph.end()
def layers(nc, k, a, out, upto, sb, dram):
    k.dis = sb("dis", [P, NB], F32)
    k.nodes.append(sb("nodes_dst", [P, TP + RING * B, 2], F32))
    k.acc = sb("acc", [P, NB, AW], F32)
    k.acc2 = sb("acc2", [P, NB, D], F32)
    k.state = sb("state", [P, NB, 2 * H], F32)
    load_weights(nc, k, a, sb)
    tables = [dram(f"scaled{n}", [NP, D]) for n in range(3)]
    agg3, rest, x2 = dram("agg3", [NP, D]), dram("rest", [NP, D]), dram("x2", [NP, D])
    a2 = dram("a2", [NP, H])
    att, p_table, out_table = dram("att", [NP, AW]), dram("p_table", [NP, D]), dram("out_table", [NP, D])
    scale_nodes(nc, k, k.x_pad, tables[0])
    hop(nc, k, tables[0], k.by_src, agg3, tables[1])
    hop(nc, k, tables[1], None, None, tables[2])
    hop(nc, k, tables[2], None, None, None)
    if upto >= 3:
        to_attention(nc, k, tables[2], k.x_pad, att, a2, rest)
    if upto >= 4:
        greatest(nc, k, a2)
        attention(nc, k, att)
        to_messages(nc, k, rest, x2, p_table)
    if upto >= 5:
        messages(nc, k, p_table)
        finish(nc, k, x2, agg3, out_table, out)


class Store:
    pass


def build(nc, a, out, upto=99):
    k = Store()
    with ExitStack() as ctx:
        def sb(name, shape, dt):
            return ctx.enter_context(nc.sbuf_tensor(name, shape, dt))

        def dram(name, shape, dt=F32):
            return nc.dram_tensor(name, shape, dt, kind="Internal").ap()

        k.ident = sb("ident", [P, P], F32)
        k.ones = sb("ones", [P, P], F32)
        k.tri = sb("tri", [P, P], F32)
        k.lanes_i = sb("lanes_i", [P, P], I32)
        k.lanes = sb("lanes", [P, P], F32)
        k.lanes_b = sb("lanes_b", [P, P], BF16)
        k.zero_b = sb("zero_b", [P, P], BF16)
        k.tile_block = [sb("tile_block_src", [1, TP], I32), sb("tile_block_dst", [1, TP], I32)]
        k.dis2 = sb("dis2", [P, NB], F32)
        k.nodes = [sb("nodes_src", [P, TP + RING * B, 2], F32)]
        k.by_src = dram("by_src", [TP * P, D + 2])
        k.by_dst = dram("by_dst", [TP * P, DE + 2])
        k.x_pad = dram("x_pad", [NP, D])
        with ExitStack() as early:
            k.tiles_i = early.enter_context(nc.sbuf_tensor("tiles_i", [P, TP], I32))
            k.tiles = early.enter_context(nc.sbuf_tensor("tiles", [P, TP], F32))
            constants(nc, k)
            group_edges(nc, k, a["src"], a["dst"], a["edge_attr_128"], a["edge_attr_32"], a["x"])
        if upto >= 2:
            layers(nc, k, a, out, upto, sb, dram)


_INS = ['x', 'src', 'dst', 'edge_attr_128', 'edge_attr_32', 'L1_gnn_W_l', 'L1_gnn_W_r', 'L1_gnn_a1w', 'L1_gnn_a2w',
        'L1_gnn_bias', 'L2_gnn_W1', 'L2_gnn_b1', 'L2_gnn_W2', 'L2_gnn_b2', 'L2_gnn_Wu', 'L2_gnn_bu', 'L2_gnn_gamma',
        'L2_gnn_beta', 'L3_gnn_W1', 'L3_gnn_b1', 'L3_gnn_W2', 'L3_gnn_b2', 'L3_gnn_ln_gamma', 'L3_gnn_ln_beta']


def kernel(**inputs):
    import numpy as _np
    import concourse.bacc as _bacc
    from concourse import mybir as _mybir
    from concourse.bass_utils import run_bass_kernel_spmd as _run

    nc = _bacc.Bacc("TRN2", target_bir_lowering=False, num_devices=1)
    arrays, args = {}, {}
    for name in _INS:
        a = _np.ascontiguousarray(inputs[name])
        arrays[f"in_{name}_dram"] = a
        args[name] = nc.dram_tensor(f"in_{name}_dram", a.shape, _mybir.dt.from_np(a.dtype), kind="ExternalInput").ap()
    out = nc.dram_tensor("out_0_dram", (N, D), F32, kind="ExternalOutput").ap()
    build(nc, args, out)
    r = _run(nc, [arrays], core_ids=[0])
    return r.results[0]["out_0_dram"]
```
